# Optimizing a Trainium2 kernel written in Bass

```python
import numpy as np
import jax
import jax.numpy as jnp

def _softmax(x, axis=-1):
    return jax.nn.softmax(x, axis=axis)

def _gelu(x):
    return jax.nn.gelu(x, approximate=True)

def _silu(x):
    return jax.nn.silu(x)

def _sigmoid(x):
    return jax.nn.sigmoid(x)

def _layernorm(x, axis=-1, eps=1e-05):
    m = jnp.mean(x, axis=axis, keepdims=True)
    v = jnp.var(x, axis=axis, keepdims=True)
    return (x - m) / jnp.sqrt(v + eps)

def _scatter_add(tgt, idx, src, axis=0):
    return tgt.at[idx].add(src)

def _segment_sum(src, seg, n):
    return jax.ops.segment_sum(src, seg, n)
kernel_name = 'mk_prb_d1_jaxref_r4_b0a03f'

def setup_inputs(seed: int=0):
    np.random.seed(seed)
    _w = jnp.asarray

    def _L0_attn_setup():
        import jax, jax.numpy as jnp
        import numpy as np
        DIM = 256
        HEADS = 16
        HEAD_DIM = DIM // HEADS

        def _xavier(key, shape):
            fan_out, fan_in = shape
            limit = float(np.sqrt(6.0 / (fan_in + fan_out)))
            return jax.random.uniform(key, shape, jnp.float32, -limit, limit)
        key = jax.random.key(seed)
        kx, kv, kk, kq = jax.random.split(key, 4)
        x = jax.random.normal(kx, (4, 512, DIM), jnp.float32)
        Wv = _xavier(kv, (DIM, DIM))
        Wk = _xavier(kk, (DIM, DIM))
        Wq = _xavier(kq, (DIM, DIM))
        return {'x': x, 'Wq': Wq, 'Wk': Wk, 'Wv': Wv}
    _L0_attn_in = _L0_attn_setup()

    def _L0_ffn_setup():
        import jax, jax.numpy as jnp
        import numpy as np
        from jax import lax
        D = 256
        H = 352
        E = 8
        K = 2
        ROUTER_SCALE = 1.0

        def _expert(x, w1, b1, w3, b3, w2, b2):
            h = jax.nn.silu((x @ w1 + b1) * (x @ w3 + b3))
            return h @ w2 + b2
        key = jax.random.key(seed)
        ks = jax.random.split(key, 16)
        s = 0.02
        inp = {'x': jax.random.normal(ks[0], (2, 512, D), dtype=jnp.float32), 'gate_w': jax.random.normal(ks[1], (E, D), dtype=jnp.float32) * s, 'gate_b': jax.random.normal(ks[2], (E,), dtype=jnp.float32) * s, 'w1': jax.random.normal(ks[3], (E, D, H), dtype=jnp.float32) * s, 'b1': jax.random.normal(ks[4], (E, H), dtype=jnp.float32) * s, 'w3': jax.random.normal(ks[5], (E, D, H), dtype=jnp.float32) * s, 'b3': jax.random.normal(ks[6], (E, H), dtype=jnp.float32) * s, 'w2': jax.random.normal(ks[7], (E, H, D), dtype=jnp.float32) * s, 'b2': jax.random.normal(ks[8], (E, D), dtype=jnp.float32) * s, 'sw1': jax.random.normal(ks[9], (D, H), dtype=jnp.float32) * s, 'sb1': jax.random.normal(ks[10], (H,), dtype=jnp.float32) * s, 'sw3': jax.random.normal(ks[11], (D, H), dtype=jnp.float32) * s, 'sb3': jax.random.normal(ks[12], (H,), dtype=jnp.float32) * s, 'sw2': jax.random.normal(ks[13], (H, D), dtype=jnp.float32) * s, 'sb2': jax.random.normal(ks[14], (D,), dtype=jnp.float32) * s}
        return inp
    _L0_ffn_in = _L0_ffn_setup()
    _d = {'L0_attn_x': _L0_attn_in['x'], 'L0_attn_Wq': _L0_attn_in['Wq'], 'L0_attn_Wk': _L0_attn_in['Wk'], 'L0_attn_Wv': _L0_attn_in['Wv'], 'L0_ffn_gate_w': _L0_ffn_in['gate_w'], 'L0_ffn_gate_b': _L0_ffn_in['gate_b'], 'L0_ffn_w1': _L0_ffn_in['w1'], 'L0_ffn_b1': _L0_ffn_in['b1'], 'L0_ffn_w3': _L0_ffn_in['w3'], 'L0_ffn_b3': _L0_ffn_in['b3'], 'L0_ffn_w2': _L0_ffn_in['w2'], 'L0_ffn_b2': _L0_ffn_in['b2'], 'L0_ffn_sw1': _L0_ffn_in['sw1'], 'L0_ffn_sb1': _L0_ffn_in['sb1'], 'L0_ffn_sw3': _L0_ffn_in['sw3'], 'L0_ffn_sb3': _L0_ffn_in['sb3'], 'L0_ffn_sw2': _L0_ffn_in['sw2'], 'L0_ffn_sb2': _L0_ffn_in['sb2']}
    _x0 = _d['L0_attn_x']
    _d['L0_attn_x'] = jax.random.normal(jax.random.fold_in(jax.random.key(seed), 1), (1, 4096, 256), dtype=_x0.dtype)
    del _x0
    return _d

def reference(L0_attn_x, L0_attn_Wq, L0_attn_Wk, L0_attn_Wv, L0_ffn_gate_w, L0_ffn_gate_b, L0_ffn_w1, L0_ffn_b1, L0_ffn_w3, L0_ffn_b3, L0_ffn_w2, L0_ffn_b2, L0_ffn_sw1, L0_ffn_sb1, L0_ffn_sw3, L0_ffn_sb3, L0_ffn_sw2, L0_ffn_sb2):

    def _L0_attn_ref(x, Wq, Wk, Wv):
        import jax, jax.numpy as jnp
        import numpy as np
        DIM = 256
        HEADS = 16
        HEAD_DIM = DIM // HEADS

        def _xavier(key, shape):
            fan_out, fan_in = shape
            limit = float(np.sqrt(6.0 / (fan_in + fan_out)))
            return jax.random.uniform(key, shape, jnp.float32, -limit, limit)
        B, S, D = x.shape
        H, Hd = (HEADS, HEAD_DIM)
        q = (x @ Wq.T).reshape(B, S, H, Hd)
        k = (x @ Wk.T).reshape(B, S, H, Hd)
        v = (x @ Wv.T).reshape(B, S, H, Hd)
        energy = jnp.einsum('bqhd,bkhd->bhqk', q, k)
        attn = jax.nn.softmax(energy / jnp.sqrt(jnp.float32(D)), axis=-1)
        out = jnp.einsum('bhqk,bkhd->bqhd', attn, v).reshape(B, S, D)
        return out

    def _L0_ffn_ref(x, gate_w, gate_b, w1, b1, w3, b3, w2, b2, sw1, sb1, sw3, sb3, sw2, sb2):
        import jax, jax.numpy as jnp
        import numpy as np
        from jax import lax
        D = 256
        H = 352
        E = 8
        K = 2
        ROUTER_SCALE = 1.0

        def _expert(x, w1, b1, w3, b3, w2, b2):
            h = jax.nn.silu((x @ w1 + b1) * (x @ w3 + b3))
            return h @ w2 + b2
        shape = x.shape
        xf = x.reshape(-1, D)
        T = xf.shape[0]
        scores = jax.nn.softmax(xf @ gate_w.T, axis=-1)
        biased = scores + gate_b
        _, idx = lax.top_k(biased, K)
        w = jnp.take_along_axis(scores, idx, axis=-1) * ROUTER_SCALE
        rw = jnp.zeros((T, E), dtype=xf.dtype).at[jnp.arange(T)[:, None], idx].add(w)
        h = jax.nn.silu((jnp.einsum('td,edh->teh', xf, w1) + b1) * (jnp.einsum('td,edh->teh', xf, w3) + b3))
        oe = jnp.einsum('teh,ehd->ted', h, w2) + b2
        y = jnp.einsum('te,ted->td', rw, oe)
        z = _expert(xf, sw1, sb1, sw3, sb3, sw2, sb2)
        return (y + z).reshape(shape)
    x = L0_attn_x
    xn = _layernorm(x, axis=-1)
    x = x + _L0_attn_ref(xn, L0_attn_Wq, L0_attn_Wk, L0_attn_Wv) + _L0_ffn_ref(xn, L0_ffn_gate_w, L0_ffn_gate_b, L0_ffn_w1, L0_ffn_b1, L0_ffn_w3, L0_ffn_b3, L0_ffn_w2, L0_ffn_b2, L0_ffn_sw1, L0_ffn_sb1, L0_ffn_sw3, L0_ffn_sb3, L0_ffn_sw2, L0_ffn_sb2)
    return x

_drawn_inputs = setup_inputs


def setup_inputs(seed=0):
    import zlib

    import numpy as np

    out = dict(_drawn_inputs(seed))
    spreads = {}
    factors = {'L0_attn_Wq': 3.324,
     'L0_attn_Wk': 3.316,
     'L0_ffn_gate_w': 8.0,
     'L0_ffn_gate_b': 8.0,
     'L0_ffn_w1': 8.0,
     'L0_ffn_b1': 8.0,
     'L0_ffn_w3': 8.0,
     'L0_ffn_b3': 8.0,
     'L0_ffn_w2': 8.0,
     'L0_ffn_b2': 39.977,
     'L0_ffn_sw1': 2.908,
     'L0_ffn_sb1': 42.794,
     'L0_ffn_sw3': 2.891,
     'L0_ffn_sb3': 45.357,
     'L0_ffn_sw2': 2.897,
     'L0_ffn_sb2': 23.328}
    for name, (base, spread) in spreads.items():
        noise = np.random.default_rng([zlib.crc32(name.encode()), seed]).standard_normal(out[name].shape)
        drawn = base * np.exp(spread * noise) if base else spread * noise
        out[name] = jnp.asarray(drawn.astype(out[name].dtype))
    for name, factor in factors.items():
        out[name] = (out[name] * factor).astype(out[name].dtype)
    return out
```

```python
import concourse.bass as bass
from concourse import mybir
from contextlib import ExitStack

T = 4096
D = 256
H = 16
HD = D // H
E = 8
NS = E + 1
F = 352
P = 128
EPS = 1e-5
NT = T // P
CH = 512
NCH = T // CH
TPC = CH // P
DT = D // P
NJ = 2 * DT
NP_ = 3
PAIRS = [(0, 0), (0, 1), (1, 0), (1, 1), (0, 2), (2, 0)]
SROW = HD * len(PAIRS)
ROWS = SROW + NP_
ENERGY_SCALE = 1.0 / 16.0
BOUND_LIMIT = 40.0 * 16.0
GK = 3
NG = -(-NT // GK)
GI = 2 * NG
NPB = 5
NB = NT // 4
ITERS = H * NCH // 2
VC = HD + 1
VW = 32
FT = [128, 128, 96]
STACK_DMAS = 2 * len(PAIRS) + 1
WHALF = 2 * DT * F + 3 * D


def slot_of_group():
    slots, left = [], GI
    while left:
        n = 5 if left % 4 else 4
        slots += list(range(n))
        left -= n
    return slots


SLOT = slot_of_group()


def layer_program(nc, x, wqT, wkT, wvT, gT, gate_b, w1, w3, w2, b1c, b3c, b2, ident, esum, hones, out):
    f32 = mybir.dt.float32
    bf16 = mybir.dt.bfloat16
    i32 = mybir.dt.int32
    ALU = mybir.AluOpType
    ACT = mybir.ActivationFunctionType
    AX = mybir.AxisListType.X
    ds = bass.ds

    ctx = ExitStack()
    with ctx:
        def sb(name, shape, dt):
            return ctx.enter_context(nc.sbuf_tensor(name, shape, dt))

        def sem(name):
            return ctx.enter_context(nc.semaphore(name))

        qk_parts = nc.dram_tensor("qk_parts", (NP_, 2 * D, T), bf16, kind="Internal").ap()
        shift_parts = nc.dram_tensor("shift_parts", (NP_, H, T), bf16, kind="Internal").ap()

        resid = sb("resid", [P, NT, D], f32)
        xnT = sb("xnT", [P, DT, T], f32)
        v_all = sb("v_all", [P, NT, H * VC + VW - VC], f32)
        q_stack = sb("q_stack", [P, 2 * T], bf16)
        k_stack = sb("k_stack", [P, 2 * T], bf16)
        probs = sb("probs", [P, NPB, GK * CH], f32)
        v_head = sb("v_head", [P, 2, NT, VW], f32)
        o_sb = sb("o_sb", [P, 2, CH], f32)
        spare = sb("spare", [P, 4608], f32)
        ident_sb = sb("ident_sb", [P, P], f32)
        esum_sb = sb("esum_sb", [P, VC], f32)
        hones_sb = sb("hones_sb", [P, DT, H], f32)
        gT_sb = sb("gT_sb", [P, DT, E], f32)
        gb_sb = sb("gb_sb", [P, E], f32)
        b1_sb = sb("b1_sb", [P, NS * 3], f32)
        b3_sb = sb("b3_sb", [P, NS * 3], f32)
        stats = sb("stats", [P, NT, 6], f32)
        mv = sb("mv", [P, NT, 2], f32)
        rstd = sb("rstd", [P, NT], f32)
        ln_t = sb("ln_t", [P, 3, NT], f32)
        rw = sb("rw", [P, NT, NS], f32)
        logits = sb("logits", [P, NT, E], f32)
        rt = sb("rt", [P, 4, NT, E], f32)
        rs = sb("rs", [P, 3, NT], f32)
        descend = sb("descend", [P, E], f32)
        rec = sb("rec", [P, 2, TPC], f32)
        o_n = sb("o_n", [P, 2, TPC, HD], f32)
        kmax = sb("kmax", [H, NCH + 2], f32)
        guard = sb("guard", [H, 4], f32)
        flag_f = sb("flag_f", [1, 4], f32)
        flag_i = sb("flag_i", [1, 1], i32)
        gmax = sb("gmax", [P, 2], f32)
        nmax = sb("nmax", [P, NT, H], f32)

        qf = q_stack[:, :].bitcast(f32)
        kf = k_stack[:, :].bitcast(f32)
        xn = qf[:, 0:TPC * D].rearrange("p (t d) -> p t d", t=TPC)
        xc = qf[:, 1024:2048].rearrange("p (t n) -> p t n", t=DT)
        resd = qf[:, 2048:4096].rearrange("p (j n) -> p j n", j=NJ)
        sq = kf[:, 0:2048].rearrange("p (j n) -> p j n", j=NJ)
        wqkv = kf[:, 2048:2048 + 3 * DT * D].rearrange("p (w t n) -> p w t n", w=3, t=DT)
        part = spare[:, 0:3072].bitcast(bf16).rearrange("p (s j n) -> p s j n", s=NP_, j=NJ)
        pflat = probs[:, :, :].rearrange("p a b -> p (a b)")
        nq = pflat[0:H, 0:T]
        sres = pflat[0:H, T:T + T // 2]
        spart = spare[0:H, 0:3072].bitcast(bf16).rearrange("p (s n) -> p s n", s=NP_)
        w13_sb = [pflat[:, s * WHALF:s * WHALF + 2 * DT * F].rearrange("p (w t n) -> p w t n", w=2, t=DT)
                  for s in range(2)]
        w2_sb = [pflat[:, s * WHALF + 2 * DT * F:(s + 1) * WHALF].rearrange("p (t n) -> p t n", t=3)
                 for s in range(2)]
        gate_in = spare[:, 0:1024].rearrange("p (a n) -> p a n", a=2)
        prod = spare[:, 1024:2048].rearrange("p (a n) -> p a n", a=2)
        hid = spare[:, 2048:3584].rearrange("p (a n) -> p a n", a=3)

        PS = ctx.enter_context(nc.psum_tensor("PS", [P, 8 * CH], f32))

        def bank(b, n=1):
            return PS[:, b * CH:(b + n) * CH]

        s_pass = sem("s_pass")
        s_const = sem("s_const")
        s_x = [sem(f"s_x{i}") for i in range(4)]
        s_dve = sem("s_dve")
        s_var = sem("s_var")
        s_std = sem("s_std")
        s_xn = sem("s_xn")
        s_tr = sem("s_tr")
        s_xc = sem("s_xc")
        s_xg = sem("s_xg")
        s_qk = sem("s_qk")
        s_hi = sem("s_hi")
        s_sq = sem("s_sq")
        s_res = sem("s_res")
        s_p2 = sem("s_p2")
        s_p3 = sem("s_p3")
        s_store = sem("s_store")
        s_v = sem("s_v")
        s_vc = sem("s_vc")
        s_lg = sem("s_lg")
        s_rt = sem("s_rt")
        s_nr = sem("s_nr")
        s_nm = sem("s_nm")
        s_mk = sem("s_mk")
        s_bound = sem("s_bound")
        s_grow = sem("s_grow")
        s_gcol = sem("s_gcol")
        s_flag = sem("s_flag")
        s_gload = sem("s_gload")
        s_gs = sem("s_gs")
        s_gr = sem("s_gr")
        s_gneg = sem("s_gneg")
        s_gt = sem("s_gt")
        s_gc = sem("s_gc")
        s_loop = sem("s_loop")
        s_shift = sem("s_shift")
        s_sst = sem("s_sst")
        s_ones = sem("s_ones")
        s_stack = sem("s_stack")
        s_lg_e = sem("s_lg_e")
        s_lg_m = sem("s_lg_m")
        s_scores = sem("s_scores")
        s_exp = sem("s_exp")
        s_vh = sem("s_vh")
        s_pv = sem("s_pv")
        s_osb = sem("s_osb")
        s_red = sem("s_red")
        s_norm = sem("s_norm")
        s_loop_a = sem("s_loop_a")
        s_w = [sem("s_w0"), sem("s_w1")]
        s_ab = sem("s_ab")
        s_gin = sem("s_gin")
        s_prod = sem("s_prod")
        s_hid = sem("s_hid")
        s_y = sem("s_y")
        s_acc = sem("s_acc")
        s_one = sem("s_one")
        s_out = sem("s_out")

        x_v = x[0].rearrange("(a p) d -> p a d", p=P)
        out_v = out[0].rearrange("(a p) d -> p a d", p=P)
        store_v = qk_parts.rearrange("s (j p) t -> s p j t", p=P)
        N_CONST = 10

        block = ctx.enter_context(nc.Block())

        @block.sync
        def _(sp):
            for i in range(4):
                sp.dma_start(resid[:, 8 * i:8 * i + 8, :], x_v[:, 8 * i:8 * i + 8, :]).then_inc(s_x[i], 16)
            for w, src in enumerate((wqT, wkT, wvT)):
                sp.dma_start(wqkv[:, w, :, :], src.rearrange("(t p) n -> p t n", p=P)).then_inc(s_const, 16)
            sp.dma_start(ident_sb[:, :], ident).then_inc(s_const, 16)
            sp.dma_start(gT_sb[:, :, :], gT.rearrange("(t p) n -> p t n", p=P)).then_inc(s_const, 16)
            sp.dma_start(hones_sb[:, :, :], hones).then_inc(s_const, 16)
            sp.dma_start(esum_sb[:, :], esum).then_inc(s_const, 16)
            sp.dma_start(gb_sb[:, :], gate_b.partition_broadcast(P)).then_inc(s_const, 16)
            sp.dma_start(b1_sb[:, :], b1c).then_inc(s_const, 16)
            sp.dma_start(b3_sb[:, :], b3c).then_inc(s_const, 16)
            with sp.Fori(0, NCH) as c:
                for s, ready in enumerate((s_hi, s_p2, s_p3)):
                    sp.wait_ge(ready, c * NJ + NJ)
                    sp.dma_start(store_v[s][:, :, ds(c * CH, CH)], part[:, s, :, :]).then_inc(s_store, 16)

            def load_stack(h, half):
                for g, (a, b) in enumerate(PAIRS):
                    sp.dma_start(q_stack[g * HD:(g + 1) * HD, ds(half * T, T)],
                                 qk_parts[a, ds(h * HD, HD), :]).then_inc(s_stack_now[0], 16)
                    sp.dma_start(k_stack[g * HD:(g + 1) * HD, ds(half * T, T)],
                                 qk_parts[b, ds(D + h * HD, HD), :]).then_inc(s_stack_now[0], 16)

            s_stack_now = [s_gload]
            sp.wait_ge(s_store, 16 * NP_ * NCH)
            sp.wait_ge(s_flag, 1)
            flag = sp.value_load(flag_i[0:1, 0:1], min_val=0, max_val=1)
            with sp.If(flag):
                with sp.Fori(0, H) as h:
                    sp.wait_ge(s_gs, h * (2 * NT))
                    sp.sem_inc(s_pass, 1)
                    load_stack(h, 0)
                    sp.wait_ge(s_gload, h * (32 * len(PAIRS)) + 32 * len(PAIRS))
                    sp.sem_inc(s_pass, 1)
            for i in range(2):
                sp.wait_ge(s_shift, i + 1)
                sp.dma_start(shift_parts[:, :, i * (T // 2):(i + 1) * (T // 2)].rearrange("s h t -> h s t"),
                             spart).then_inc(s_sst, 16)
            sp.wait_ge(s_sst, 32)
            sp.wait_ge(s_ones, 1)
            s_stack_now[0] = s_stack

            def load_head(h, half):
                load_stack(h, half)
                sp.dma_start(q_stack[SROW:ROWS, ds(half * T, T)],
                             shift_parts[:, ds(h, 1), :].rearrange("s h t -> (s h) t")).then_inc(s_stack, 16)

            load_head(0, 0)
            sp.wait_ge(s_stack, 16 * STACK_DMAS)
            load_head(1, 1)
            with sp.Fori(2, H) as h:
                sp.wait_ge(s_stack, h * (16 * STACK_DMAS))
                sp.wait_ge(s_scores, h * (4 * GI) - 4 * GI)
                sp.sem_inc(s_pass, 1)
                load_head(h, h % 2)

            def load_expert(s, half):
                sp.dma_start(w13_sb[half][:, 0, :, :],
                             w1[ds(s, 1), :, :].rearrange("e (t p) n -> p (e t) n", p=P)).then_inc(s_w[half], 16)
                sp.dma_start(w13_sb[half][:, 1, :, :],
                             w3[ds(s, 1), :, :].rearrange("e (t p) n -> p (e t) n", p=P)).then_inc(s_w[half], 16)
                sp.dma_start(w2_sb[half][:, 0:2, :],
                             w2[ds(s, 1), 0:2 * P, :].rearrange("e (t p) n -> p (e t) n", p=P)).then_inc(s_w[half], 16)
                sp.dma_start(w2_sb[half][0:FT[2], 2, :],
                             w2[ds(s, 1), 2 * P:F, :].rearrange("e p n -> (e p) n")).then_inc(s_w[half], 16)
                sp.dma_start(w2_sb[half][FT[2]:FT[2] + 1, 2, :], b2[ds(s, 1), :]).then_inc(s_w[half], 16)

            sp.wait_ge(s_pv, H * NCH)
            load_expert(0, 1)
            load_expert(1, 0)
            with sp.Fori(1, E // 2) as p:
                sp.wait_ge(s_y, p * (2 * NCH) - NCH)
                sp.sem_inc(s_pass, 1)
                load_expert(p * 2, 1)
                sp.wait_ge(s_y, p * (2 * NCH))
                sp.sem_inc(s_pass, 1)
                load_expert(p * 2 + 1, 0)
            sp.wait_ge(s_y, E * NCH - NCH)
            load_expert(E, 1)
            with sp.Fori(0, NCH) as c:
                sp.wait_ge(s_acc, c + (E * NCH + 1))
                sp.sem_inc(s_pass, 1)
                sp.dma_start(out_v[:, ds(c * TPC, TPC), :], resid[:, ds(c * TPC, TPC), :]).then_inc(s_out, 16)
            sp.wait_ge(s_out, 16 * NCH)

        @block.tensor
        def _(pe):
            pe.wait_ge(s_const, 16 * N_CONST)
            with pe.Fori(0, NCH) as c:
                pe.wait_ge(s_xn, c + 1)
                pe.wait_ge(s_vc, c * 2)
                for dt in range(DT):
                    for t in range(TPC):
                        last = pe.transpose(bank(dt)[:, t * P:(t + 1) * P], xn[:, t, dt * P:(dt + 1) * P], ident_sb[:, :])
                last.then_inc(s_tr, 1)
                pe.wait_ge(s_xc, c + 1)
                pe.wait_ge(s_res, c * NJ)
                pe.wait_ge(s_sq, c * NJ)
                for j in range(NJ):
                    for dt in range(DT):
                        last = pe.matmul(bank(2 + j), wqkv[:, j // DT, dt, (j % DT) * P:(j % DT + 1) * P], xc[:, dt, :],
                                         start=(dt == 0), stop=(dt == DT - 1))
                    last.then_inc(s_qk, 1)
                for t in range(TPC):
                    for dt in range(DT):
                        last = pe.matmul(bank(t // 2)[:, (t % 2) * D:(t % 2 + 1) * D], xc[:, dt, t * P:(t + 1) * P],
                                         wqkv[:, 2, dt, :], start=(dt == 0), stop=(dt == DT - 1))
                    if t % 2:
                        last.then_inc(s_v, 1)
                pe.wait_ge(s_rt, c)
                for t in range(TPC):
                    for dt in range(DT):
                        last = pe.matmul(bank(6)[:, t * E:(t + 1) * E], xc[:, dt, t * P:(t + 1) * P], gT_sb[:, dt, :],
                                         start=(dt == 0), stop=(dt == DT - 1))
                last.then_inc(s_lg, 1)
                pe.wait_ge(s_nm, c)
                pe.wait_ge(s_sq, c * NJ + NJ)
                for w in range(2):
                    for dt in range(DT):
                        last = pe.matmul(bank(7)[32 * w:32 * w + H, :], hones_sb[:, dt, :], sq[:, w * DT + dt, :],
                                         start=(dt == 0), stop=(dt == DT - 1))
                last.then_inc(s_nr, 1)
            pe.wait_ge(s_gcol, 1)
            pe.transpose(bank(0)[0:1, 0:H], guard[:, 0:1], ident_sb[0:H, 0:H]).then_inc(s_grow, 1)
            pe.wait_ge(s_flag, 1)
            flag = pe.value_load(flag_i[0:1, 0:1], min_val=0, max_val=1)
            with pe.If(flag):
                with pe.Fori(0, H) as h:
                    pe.wait_ge(s_gload, h * (32 * len(PAIRS)) + 32 * len(PAIRS))
                    pe.sem_inc(s_pass, 1)
                    with pe.Fori(0, NT) as t:
                        for half in range(2):
                            pe.wait_ge(s_gr, h * (2 * NT) + t * 2)
                            for n in range(4):
                                col = (4 * half + n) * CH
                                last = pe.matmul(bank(4 * half + n), q_stack[0:SROW, ds(t * P, P)], k_stack[0:SROW, col:col + CH],
                                                 start=True, stop=True)
                            last.then_inc(s_gs, 1)
                pe.wait_ge(s_gneg, 1)
                for t in range(NT):
                    last = pe.transpose(PS[0:H, t * P:(t + 1) * P], nmax[:, t, :], ident_sb[:, :])
                last.then_inc(s_gt, 1)

            def scores(it, g):
                c, lo = g // NG, (g % NG) * GK
                qcol = (it * (2 * CH) + c * CH) % (2 * T)
                kcol = (it // (NCH // 2)) % 2 * T
                for n, kt in enumerate(range(lo, min(lo + GK, NT))):
                    last = pe.matmul(bank(GK * (g % 2) + n), k_stack[0:ROWS, ds(kcol + kt * P, P)],
                                     q_stack[0:ROWS, ds(qcol, CH)], start=True, stop=True)
                last.then_inc(s_scores, 1)

            def values(c, b):
                for j in range(4):
                    kt = 4 * b + j
                    slot = SLOT[c * NG + kt // GK]
                    last = pe.matmul(bank(6 + c)[VW * j:VW * (j + 1), :], v_head[:, c, kt, :],
                                     probs[:, slot, (kt % GK) * CH:(kt % GK + 1) * CH], start=(b == 0), stop=(b == NB - 1))
                if b == NB - 1:
                    last.then_inc(s_pv, 1)

            def reduce(c, n):
                pe.wait_ge(s_osb, n + 1)
                for t in range(TPC):
                    last = pe.matmul(bank(6 + c)[:, t * VC:(t + 1) * VC], o_sb[:, c, t * P:(t + 1) * P], esum_sb[:, :],
                                     start=True, stop=True)
                last.then_inc(s_red, 1)

            def iteration(it, first, last):
                for g in range(GI):
                    c, gg = g // NG, g % NG
                    n = it * 2 + c
                    pe.wait_ge(s_exp, it * GI + g + 1)
                    if g + 2 < GI:
                        scores(it, g + 2)
                    elif not last:
                        if g + 2 == GI:
                            pe.wait_ge(s_stack, ((it + 1) // (NCH // 2)) * (16 * STACK_DMAS) + 16 * STACK_DMAS)
                        scores(it + 1, g + 2 - GI)
                    for b in range(NB):
                        if (4 * b + 3) // GK == gg:
                            if b == 0:
                                pe.wait_ge(s_vh, n + 1)
                                if not (first and c == 0):
                                    pe.wait_ge(s_norm, n - 1)
                            values(c, b)
                    if gg == 3 and not (first and c == 0):
                        reduce(1 - c, n - 1)

            pe.wait_ge(s_stack, 16 * STACK_DMAS)
            scores(0, 0)
            scores(0, 1)
            iteration(0, True, False)
            with pe.Fori(1, ITERS - 1) as it:
                iteration(it, False, False)
            iteration(ITERS - 1, False, True)
            reduce(1, H * NCH - 1)

            def up(half, a, j, m):
                pe.wait_ge(s_prod, m * 3)
                for w in range(2):
                    for dt in range(DT):
                        last = pe.matmul(bank(3 * w + j)[0:FT[j], :], w13_sb[half][:, w, dt, j * P:j * P + FT[j]],
                                         xnT[:, dt, ds(a * CH, CH)], start=(dt == 0), stop=(dt == DT - 1))
                last.then_inc(s_ab, 1)

            def down(half, m):
                pe.wait_ge(s_hid, m * 3 + 3)
                pe.wait_ge(s_acc, m)
                for t in range(TPC):
                    for j in range(3):
                        rows = FT[j] + (j == 2)
                        last = pe.matmul(bank(6 + t // 2)[:, (t % 2) * D:(t % 2 + 1) * D], hid[0:rows, j, t * P:(t + 1) * P],
                                         w2_sb[half][0:rows, j, :], start=(j == 0), stop=(j == 2))
                last.then_inc(s_y, 1)

            def chunk(half, half_before, a, m, first=False):
                up(half, a, 0, m)
                if not first:
                    down(half_before, m - 1)
                up(half, a, 1, m)
                up(half, a, 2, m)

            pe.wait_ge(s_norm, H * NCH)
            pe.wait_ge(s_one, 1)
            pe.wait_ge(s_w[1], 80)
            chunk(1, 1, 0, 0, first=True)
            with pe.Fori(1, NCH) as a:
                chunk(1, 1, a, a)
            with pe.Fori(0, E // 2) as p:
                pe.wait_ge(s_w[0], p * 80 + 80)
                pe.sem_inc(s_pass, 1)
                chunk(0, 1, 0, p * (2 * NCH) + NCH)
                with pe.Fori(1, NCH) as a:
                    chunk(0, 0, a, p * (2 * NCH) + NCH + a)
                pe.wait_ge(s_w[1], p * 80 + 160)
                pe.sem_inc(s_pass, 1)
                chunk(1, 0, 0, p * (2 * NCH) + 2 * NCH)
                with pe.Fori(1, NCH) as a:
                    chunk(1, 1, a, p * (2 * NCH) + 2 * NCH + a)
            down(1, NS * NCH - 1)

        @block.scalar
        def _(act):
            act.wait_ge(s_var, 1)
            nc.scalar.activation(ln_t[:, 1, :], ln_t[:, 0, :], ACT.Sqrt).then_inc(s_std, 1)
            with act.Fori(0, NCH) as c:
                act.wait_ge(s_tr, c + 1)
                act.wait_ge(s_xg, c)
                nc.scalar.activation(xc[:, 0, :], bank(0), ACT.Copy)
                nc.scalar.activation(xc[:, 1, :], bank(1), ACT.Copy).then_inc(s_xc, 1)
                act.wait_ge(s_store, c * (16 * NP_))
                for j in range(NJ):
                    act.wait_ge(s_qk, c * NJ + (j + 1))
                    nc.scalar.activation(part[:, 0, j, :], bank(2 + j), ACT.Copy).then_inc(s_hi, 1)
                    nc.scalar.activation(sq[:, j, :], bank(2 + j), ACT.Square).then_inc(s_sq, 1)
            act.wait_ge(s_mk, 1)
            nc.scalar.activation(nq, nq, ACT.Sqrt, scale=kmax[:, NCH:NCH + 1]).then_inc(s_bound, 1)
            act.wait_ge(s_lg_m, 1)
            nc.scalar.activation(rt[:, 0, :, :], rt[:, 1, :, :], ACT.Exp).then_inc(s_lg_e, 1)

            def exps(it):
                for g in range(GI):
                    w = (min((g % NG) * GK + GK, NT) - (g % NG) * GK) * CH
                    act.wait_ge(s_scores, it * GI + (g + 1))
                    nc.scalar.activation(probs[:, SLOT[g], 0:w], bank(GK * (g % 2), GK)[:, 0:w], ACT.Exp,
                                         scale=ENERGY_SCALE).then_inc(s_exp, 1)

            act.wait_ge(s_shift, 3)
            with act.Fori(0, ITERS) as it:
                exps(it)

            def hidden(s, m):
                for j in range(3):
                    act.wait_ge(s_ab, m * 3 + (j + 1))
                    if j == 2:
                        act.wait_ge(s_prod, m * 3 + 1)
                    else:
                        act.wait_ge(s_prod, m * 3)
                    nc.scalar.activation(gate_in[0:FT[j], j % 2, :], bank(j)[0:FT[j], :], ACT.Identity,
                                         bias=b1_sb[0:FT[j], ds(s * 3 + j, 1)]).then_inc(s_gin, 1)
                for j in range(3):
                    act.wait_ge(s_prod, m * 3 + (j + 1))
                    if j == 0:
                        act.wait_ge(s_y, m)
                    nc.scalar.activation(hid[0:FT[j], j, :], prod[0:FT[j], j % 2, :], ACT.Silu).then_inc(s_hid, 1)

            with act.Fori(0, NS) as s:
                with act.Fori(0, NCH) as a:
                    hidden(s, s * NCH + a)

        @block.gpsimd
        def _(pool):
            with pool.Fori(0, NCH) as c:
                pool.wait_ge(s_xc, c + 1)
                nc.gpsimd.tensor_copy(xnT[:, :, ds(c * CH, CH)], xc[:, :, :]).then_inc(s_xg, 1)
                pool.wait_ge(s_store, c * (16 * NP_))
                for j in range(NJ):
                    pool.wait_ge(s_res, c * NJ + (j + 1))
                    pool.sem_inc(s_pass, 1)
                    nc.gpsimd.tensor_copy(part[:, 1, j, :], resd[:, j, :]).then_inc(s_p2, 1)
                    pool.wait_ge(s_p2, c * NJ + (j + 1))
                    nc.gpsimd.tensor_tensor(part[:, 2, j, :], resd[:, j, :], part[:, 1, j, :], ALU.subtract).then_inc(s_p3, 1)

        @block.vector
        def _(dve):
            steps = [0]

            def link(ins):
                steps[0] += 1
                ins.then_inc(s_dve, 1)
                dve.wait_ge(s_dve, steps[0])

            V = nc.vector
            V.memset(v_all[:, :, :], 1.0)
            V.memset(rw[:, :, :], 1.0)
            for e in range(E):
                last = V.memset(descend[:, e:e + 1], float(E - e))
            link(last)
            for t in range(NT):
                if t % 8 == 0:
                    dve.wait_ge(s_x[t // 8], 16)
                last = V.bn_stats(stats[:, t, :], resid[:, t, :])
            link(last)
            for t in range(NT):
                last = V.bn_aggr(mv[:, t, :], stats[:, t, :])
            link(last)
            V.tensor_scalar(ln_t[:, 0, :], mv[:, :, 1], EPS, None, ALU.add).then_inc(s_var, 1)
            dve.wait_ge(s_var, 1)
            dve.wait_ge(s_std, 1)
            link(V.reciprocal(rstd[:, :], ln_t[:, 1, :]))
            link(V.tensor_tensor(ln_t[:, 2, :], rstd[:, :], rstd[:, :], ALU.mult))
            link(V.tensor_tensor(ln_t[:, 2, :], ln_t[:, 2, :], ln_t[:, 0, :], ALU.mult))
            link(V.tensor_scalar(ln_t[:, 2, :], ln_t[:, 2, :], -0.5, 1.5, ALU.mult, ALU.add))
            link(V.tensor_tensor(rstd[:, :], rstd[:, :], ln_t[:, 2, :], ALU.mult))

            with dve.Fori(0, NCH) as c:
                dve.wait_ge(s_tr, c)
                for t in range(TPC):
                    last = V.tensor_scalar(xn[:, t, :], resid[:, ds(c * TPC + t, 1), :].rearrange("p a d -> p (a d)"),
                                           mv[:, ds(c * TPC + t, 1), 0], rstd[:, ds(c * TPC + t, 1)],
                                           ALU.subtract, ALU.mult)
                last.then_inc(s_xn, 1)
                dve.wait_ge(s_p3, c * NJ)
                for j in range(NJ):
                    dve.wait_ge(s_sq, c * NJ + (j + 1))
                    V.tensor_tensor(resd[:, j, :], bank(2 + j), part[:, 0, j, :], ALU.subtract).then_inc(s_res, 1)
                for b in range(2):
                    dve.wait_ge(s_v, c * 2 + (b + 1))
                    V.tensor_copy(v_all[:, ds(c * TPC + 2 * b, 2), 0:H * VC].rearrange("p t (h w) -> p t h w", w=VC)[:, :, :, 0:HD],
                                  bank(b).rearrange("p (t h w) -> p t h w", t=2, w=HD)).then_inc(s_vc, 1)
                dve.wait_ge(s_lg, c + 1)
                V.tensor_copy(logits[:, ds(c * TPC, TPC), :], bank(6)[:, 0:TPC * E].rearrange("p (t e) -> p t e", t=TPC)).then_inc(s_rt, 1)
                dve.wait_ge(s_nr, c + 1)
                V.tensor_copy(nq[:, ds(c * CH, CH)], bank(7)[0:H, :])
                V.reduce_max(kmax[:, ds(c, 1)], bank(7)[32:32 + H, :], axis=AX).then_inc(s_nm, 1)
            dve.wait_ge(s_nm, NCH)
            V.reduce_max(kmax[:, NCH:NCH + 1], kmax[:, 0:NCH], axis=AX).then_inc(s_mk, 1)
            dve.wait_ge(s_bound, 1)
            V.reduce_max(guard[:, 0:1], nq, axis=AX).then_inc(s_gcol, 1)
            link(V.tensor_scalar(nq, nq, -1.0, None, ALU.mult))
            dve.wait_ge(s_grow, 1)
            link(V.reduce_max(flag_f[0:1, 0:1], bank(0)[0:1, 0:H], axis=AX))
            link(V.tensor_scalar(flag_f[0:1, 1:2], flag_f[0:1, 0:1], BOUND_LIMIT, None, ALU.is_le))
            link(V.tensor_scalar(flag_f[0:1, 2:3], flag_f[0:1, 1:2], -1.0, 1.0, ALU.mult, ALU.add))
            V.tensor_copy(flag_i[0:1, 0:1], flag_f[0:1, 2:3]).then_inc(s_flag, 1)
            dve.wait_ge(s_flag, 1)
            flag = dve.value_load(flag_i[0:1, 0:1], min_val=0, max_val=1)
            with dve.If(flag):
                with dve.Fori(0, H) as h:
                    with dve.Fori(0, NT) as t:
                        for half in range(2):
                            dve.wait_ge(s_gs, h * (2 * NT) + t * 2 + (half + 1))
                            V.reduce_max(gmax[:, half:half + 1], bank(4 * half, 4), axis=AX).then_inc(s_gr, 1)
                        dve.wait_ge(s_gr, h * (2 * NT) + t * 2 + 2)
                        V.tensor_scalar(nmax[:, ds(t, 1), ds(h, 1)].rearrange("p a b -> p (a b)"), gmax[:, 0:1],
                                        gmax[:, 1:2], -1.0, ALU.max, ALU.mult).then_inc(s_loop, 1)
                        dve.wait_ge(s_loop, h * NT + t + 1)
                V.engine_nop().then_inc(s_gneg, 1)
                dve.wait_ge(s_gt, 1)
                for n in range(NCH):
                    last = V.tensor_copy(nq[:, n * CH:(n + 1) * CH], PS[0:H, n * CH:(n + 1) * CH])
                last.then_inc(s_gc, 1)
                dve.wait_ge(s_gc, 1)
            for i in range(2):
                sl = slice(i * (T // 2), (i + 1) * (T // 2))
                if i:
                    dve.wait_ge(s_sst, 16)
                else:
                    dve.wait_ge(s_store, 16 * NP_ * NCH)
                link(V.tensor_copy(spart[:, 0, :], nq[:, sl]))
                link(V.tensor_tensor(sres, nq[:, sl], spart[:, 0, :], ALU.subtract))
                link(V.tensor_copy(spart[:, 1, :], sres))
                V.tensor_tensor(spart[:, 2, :], sres, spart[:, 1, :], ALU.subtract).then_inc(s_shift, 1)
            V.memset(k_stack[SROW:ROWS, :], 1.0).then_inc(s_ones, 1)
            dve.wait_ge(s_ones, 1)

            def copy_v(c, h):
                V.tensor_copy(v_head[:, c, :, :], v_all[:, :, ds(h * VC, VW)]).then_inc(s_vh, 1)

            copy_v(0, 0)
            copy_v(1, 0)
            V.engine_nop().then_inc(s_shift, 1)

            def bc(ap):
                return ap.unsqueeze(2).to_broadcast([P, NT, E])

            lg, sc, bi, t1, t2 = logits[:, :, :], rt[:, 0, :, :], rt[:, 1, :, :], rt[:, 2, :, :], rt[:, 3, :, :]
            link(V.reduce_max(rs[:, 0, :], lg, axis=AX))
            V.tensor_tensor(bi, lg, bc(rs[:, 0, :]), ALU.subtract).then_inc(s_lg_m, 1)
            dve.wait_ge(s_lg_e, 1)
            link(V.reduce_sum(rs[:, 0, :], sc, axis=AX))
            link(V.reciprocal(rs[:, 1, :], rs[:, 0, :]))
            link(V.tensor_tensor(sc, sc, bc(rs[:, 1, :]), ALU.mult))
            link(V.tensor_tensor(bi, sc, gb_sb[:, :].unsqueeze(1).to_broadcast([P, NT, E]), ALU.add))
            down = descend[:, :].unsqueeze(1).to_broadcast([P, NT, E])
            for k in range(2):
                link(V.reduce_max(rs[:, 0, :], bi, axis=AX))
                link(V.tensor_tensor(t1, bi, bc(rs[:, 0, :]), ALU.is_equal))
                link(V.tensor_tensor(t1, t1, down, ALU.mult))
                link(V.reduce_max(rs[:, 1, :], t1, axis=AX))
                if k == 0:
                    link(V.tensor_tensor(t2, down, bc(rs[:, 1, :]), ALU.is_equal))
                    link(V.scalar_tensor_tensor(bi, t2, -3.0e38, bi, ALU.mult, ALU.add))
                else:
                    link(V.tensor_tensor(t1, down, bc(rs[:, 1, :]), ALU.is_equal))
            link(V.tensor_tensor(t1, t1, t2, ALU.add))
            link(V.tensor_tensor(rw[:, :, 1:NS], sc, t1, ALU.mult))

            with dve.Fori(0, ITERS) as it:
                for c in range(2):
                    dve.wait_ge(s_pv, it * 2 + (c + 1))
                    V.tensor_copy(o_sb[:, c, :], bank(6 + c)).then_inc(s_osb, 1)
                    copy_v(c, ((it + 1) // (NCH // 2)) % H)
                    dve.wait_ge(s_red, it * 2 + (c + 1))
                    o = bank(6 + c)[:, 0:TPC * VC].rearrange("p (t w) -> p t w", w=VC)
                    V.reciprocal(rec[:, c, :], o[:, :, HD]).then_inc(s_loop_a, 1)
                    dve.wait_ge(s_loop_a, it * 4 + (2 * c + 1))
                    V.tensor_tensor(o_n[:, c, :, :], o[:, :, 0:HD], rec[:, c, :].unsqueeze(2).to_broadcast([P, TPC, HD]),
                                    ALU.mult).then_inc(s_norm, 1)
                    dve.wait_ge(s_norm, it * 2 + (c + 1))
                    dst = resid[:, ds(((it % (NCH // 2)) * 2 + c) * TPC, TPC), ds((it // (NCH // 2)) * HD, HD)]
                    V.tensor_tensor(dst, dst, o_n[:, c, :, :], ALU.add).then_inc(s_loop_a, 1)
            dve.wait_ge(s_loop_a, ITERS * 4)
            V.memset(hid[FT[2]:FT[2] + 1, 2, :], 1.0).then_inc(s_one, 1)
            dve.wait_ge(s_one, 1)

            def products(s, a, m, first):
                for j in range(3):
                    dve.wait_ge(s_gin, m * 3 + (j + 1))
                    if not first or j == 2:
                        dve.wait_ge(s_hid, m * 3 + (j - 1))
                    V.scalar_tensor_tensor(prod[0:FT[j], j % 2, :], bank(3 + j)[0:FT[j], :], b3_sb[0:FT[j], ds(s * 3 + j, 1)],
                                           gate_in[0:FT[j], j % 2, :], ALU.add, ALU.mult).then_inc(s_prod, 1)

            def accumulate(s, a, m):
                dve.wait_ge(s_y, m + 1)
                dve.wait_ge(s_acc, m)
                for t in range(TPC):
                    row = resid[:, ds(a * TPC + t, 1), :].rearrange("p a d -> p (a d)")
                    last = V.scalar_tensor_tensor(row, bank(6 + t // 2)[:, (t % 2) * D:(t % 2 + 1) * D],
                                                  rw[:, ds(a * TPC + t, 1), ds(s, 1)].rearrange("p a b -> p (a b)"),
                                                  row, ALU.mult, ALU.add)
                last.then_inc(s_acc, 1)

            products(0, 0, 0, True)
            with dve.Fori(1, NCH * NS) as m:
                products(m // NCH, m % NCH, m, False)
                accumulate((m - 1) // NCH, (m - 1) % NCH, m - 1)
            accumulate(NS - 1, NCH - 1, NS * NCH - 1)


def kernel(**inputs):
    import numpy as np
    import concourse.bacc as bacc
    from concourse import mybir as mb
    from concourse.bass_utils import run_bass_kernel_spmd

    a = {k[3:]: np.ascontiguousarray(v) for k, v in inputs.items()}

    def columns(shared, routed):
        b = np.concatenate([shared[None], routed], 0)
        full = np.zeros((NS, 3 * P), b.dtype)
        full[:, :F] = b
        return np.ascontiguousarray(full.reshape(NS, 3, P).transpose(2, 0, 1).reshape(P, NS * 3))

    def slots(shared, routed):
        return np.concatenate([shared[None], routed], 0)

    esum = np.zeros((P, VC), np.float32)
    for g in range(P // VW):
        esum[g * VW:g * VW + VC] = np.eye(VC, dtype=np.float32)
    hones = np.zeros((P, DT, H), np.float32)
    for p in range(P):
        for t in range(DT):
            hones[p, t, t * (P // HD) + p // HD] = 1.0
    arrays = {
        "x": a["attn_x"], "wqT": np.ascontiguousarray(a["attn_Wq"].T), "wkT": np.ascontiguousarray(a["attn_Wk"].T),
        "wvT": np.ascontiguousarray(a["attn_Wv"].T), "gT": np.ascontiguousarray(a["ffn_gate_w"].T), "gate_b": a["ffn_gate_b"],
        "w1": slots(a["ffn_sw1"], a["ffn_w1"]), "w3": slots(a["ffn_sw3"], a["ffn_w3"]), "w2": slots(a["ffn_sw2"], a["ffn_w2"]),
        "b1c": columns(a["ffn_sb1"], a["ffn_b1"]), "b3c": columns(a["ffn_sb3"], a["ffn_b3"]),
        "b2": slots(a["ffn_sb2"], a["ffn_b2"]),
        "ident": np.eye(P, dtype=np.float32), "esum": esum, "hones": hones,
    }
    nc = bacc.Bacc("TRN2", target_bir_lowering=False, num_devices=1)
    aps = [nc.dram_tensor("in_" + n, v.shape, mb.dt.from_np(v.dtype), kind="ExternalInput").ap() for n, v in arrays.items()]
    out = nc.dram_tensor("out_0", (1, T, D), mb.dt.float32, kind="ExternalOutput").ap()
    layer_program(nc, *aps, out)
    r = run_bass_kernel_spmd(nc, [{"in_" + n: v for n, v in arrays.items()}], core_ids=[0])
    return r.results[0]["out_0"]
```

```python
import concourse.bass as bass
from concourse import mybir
from contextlib import ExitStack

T = 4096
D = 256
H = 16
HD = D // H
E = 8
NS = E + 1
F = 352
P = 128
EPS = 1e-5
NT = T // P
CH = 512
NCH = T // CH
TPC = CH // P
DT = D // P
NJ = 2 * DT
NP_ = 3
PAIRS = [(0, 0), (0, 1), (1, 0), (1, 1), (0, 2), (2, 0)]
SROW = HD * len(PAIRS)
ROWS = SROW + NP_
ENERGY_SCALE = 1.0 / 16.0
BOUND_LIMIT = 40.0 * 16.0
GK = 2
SB = 3
NG = -(-NT // GK)
GI = 2 * NG
NPB = 6
NB = NT // 4
ITERS = H * NCH // 2
VC = HD + 1
VW = 32
FT = [128, 128, 96]
STACK_DMAS = 2 * len(PAIRS) + 2
TOP = 2
ST = (TOP * T + E * (CH - 1)) // CH
WDMAS = 6
WHALF = 2 * DT * F + 3 * D


def slot_of_group():
    slots, left = [], GI
    while left:
        n = 6 if left % 5 else 5
        slots += list(range(n))
        left -= n
    return slots


SLOT = slot_of_group()


def score_buffer(g):
    return g % GI % SB


def made_after():
    after, step = [[] for _ in range(GI)], -1
    for g in range(SB, GI + SB):
        before = max(x for x in range(g) if score_buffer(x) == score_buffer(g))
        step = max(step, before)
        after[step].append(g)
    return after


AFTER = made_after()


def layer_program(nc, x, wqT, wkT, wvT, gT, gate_b, w1, w3, w2, b13, b2, ident, hones, prefix, ones, steps_c, out):
    f32 = mybir.dt.float32
    bf16 = mybir.dt.bfloat16
    i32 = mybir.dt.int32
    u32 = mybir.dt.uint32
    ALU = mybir.AluOpType
    ACT = mybir.ActivationFunctionType
    AX = mybir.AxisListType.X
    ds = bass.ds

    ctx = ExitStack()
    with ctx:
        def sb(name, shape, dt):
            return ctx.enter_context(nc.sbuf_tensor(name, shape, dt))

        def sem(name):
            return ctx.enter_context(nc.semaphore(name))

        qk_parts = nc.dram_tensor("qk_parts", (NP_, 2 * D, T), bf16, kind="Internal").ap()
        qshift_parts = nc.dram_tensor("qshift_parts", (NP_, H, T), bf16, kind="Internal").ap()
        kshift = nc.dram_tensor("kshift", (H, T), bf16, kind="Internal").ap()
        xn_rows = nc.dram_tensor("xn_rows", (T, D), f32, kind="Internal").ap()
        slot_x = nc.dram_tensor("slot_x", (ST * CH, D), f32, kind="Internal").ap()
        slot_y = nc.dram_tensor("slot_y", (ST * CH, D), f32, kind="Internal").ap()

        resid = sb("resid", [P, NT, D], f32)
        xnT = sb("xnT", [P, DT, T], f32)
        v_all = sb("v_all", [P, NT, H * VC + VW - VC], f32)
        q_stack = sb("q_stack", [P, 2 * T], bf16)
        k_stack = sb("k_stack", [P, 2 * T], bf16)
        probs = sb("probs", [P, NPB, GK * CH], f32)
        v_head = sb("v_head", [P, 2, NT, VW], f32)
        o_sb = sb("o_sb", [P, 2, CH], f32)
        spare = sb("spare", [P, 4608], f32)
        ident_sb = sb("ident_sb", [P, P], f32)
        hones_b = sb("hones_b", [P, DT, H], bf16)
        hones_sb = sb("hones_sb", [P, DT, H], f32)
        gT_sb = sb("gT_sb", [P, DT, E], f32)
        gb_sb = sb("gb_sb", [P, E], f32)
        prefix_sb = sb("prefix_sb", [P, P], f32)
        ones_sb = sb("ones_sb", [P, P], f32)
        steps_sb = sb("steps_sb", [P, 2 * E + ST], f32)
        bias_sb = sb("bias_sb", [P, 2, 6], f32)
        stats = sb("stats", [P, NT, 6], f32)
        mv = sb("mv", [P, NT, 2], f32)
        rstd = sb("rstd", [P, NT], f32)
        ln_t = sb("ln_t", [P, 3, NT], f32)
        logits = sb("logits", [P, NT, E], f32)
        rt = sb("rt", [P, 7, NT, E], f32)
        rs = sb("rs", [P, 3, NT], f32)
        sizes = sb("sizes", [P, 4, E], f32)
        cmp_sz = sb("cmp_sz", [P, E, E], f32)
        weight = sb("weight", [P, NT, TOP], f32)
        posf = sb("posf", [P, NT, TOP], f32)
        pos = sb("pos", [P, NT, TOP], u32)
        tile_c = sb("tile_c", [1, ST, E], f32)
        tile_f = sb("tile_f", [1, ST], f32)
        tile_slot = sb("tile_slot", [1, ST], i32)
        index_s = sb("index_s", [P, TPC, TOP], u32)
        index_g = sb("index_g", [P, TPC, TOP], u32)
        rec = sb("rec", [P, 2, TPC], f32)
        o_n = sb("o_n", [P, 2, TPC, VC], f32)
        kmax = sb("kmax", [H, NCH + 3], f32)
        qmax = sb("qmax", [H, NCH + 2], f32)
        flag_f = sb("flag_f", [1, 4], f32)
        flag_i = sb("flag_i", [1, 1], i32)
        gmax = sb("gmax", [P, 2], f32)

        qf = q_stack[:, :].bitcast(f32)
        kf = k_stack[:, :].bitcast(f32)
        xn = qf[:, 0:TPC * D].rearrange("p (t d) -> p t d", t=TPC)
        xc = qf[:, 1024:2048].rearrange("p (t n) -> p t n", t=DT)
        resd = qf[:, 2048:4096].rearrange("p (j n) -> p j n", j=NJ)
        sq = kf[:, 0:1024].bitcast(bf16).rearrange("p (j n) -> p j n", j=NJ)
        wqkv = kf[:, 2048:2048 + 3 * DT * D].rearrange("p (w t n) -> p w t n", w=3, t=DT)
        part = spare[:, 0:3072].bitcast(bf16).rearrange("p (s j n) -> p s j n", s=NP_, j=NJ)
        pflat = probs[:, :, :].rearrange("p a b -> p (a b)")
        kfill = pflat[0:H, 0:T // 2].bitcast(bf16)
        qnorm = pflat[0:H, 2048:2048 + CH]
        sres = pflat[0:H, 2560:2560 + CH]
        spart = pflat[0:H, 3072:3072 + 768].bitcast(bf16).rearrange("p (s n) -> p s n", s=NP_)
        w13_sb = [pflat[:, s * WHALF:s * WHALF + 2 * DT * F].rearrange("p (w t n) -> p w t n", w=2, t=DT)
                  for s in range(2)]
        w2_sb = [pflat[:, s * WHALF + 2 * DT * F:(s + 1) * WHALF].rearrange("p (t n) -> p t n", t=3)
                 for s in range(2)]
        gate_in = spare[:, 0:1024].rearrange("p (a n) -> p a n", a=2)
        prod = spare[:, 1024:2048].rearrange("p (a n) -> p a n", a=2)
        hid = spare[:, 2048:3584].rearrange("p (a n) -> p a n", a=3)
        xn_in = spare[:, 0:2048].rearrange("p (b t n) -> p b t n", b=2, t=TPC)
        zeros = spare[:, 2048:3072]
        nmax = spare[:, 3072:3584].rearrange("p (t h) -> p t h", t=NT)
        chosen = spare[:, 3584:3840].rearrange("p (t e) -> p t e", t=NT)
        ranks = spare[:, 3840:4352].rearrange("p (a t e) -> p a t e", a=2, t=NT)
        slot_in = qf[:, 0:2048].rearrange("p (b t n) -> p b t n", b=2, t=TPC)
        slot_T = qf[:, 2048:4096].rearrange("p (b t n) -> p b t n", b=2, t=DT)
        y_sb = kf[:, 0:2048].rearrange("p (b t n) -> p b t n", b=2, t=TPC)
        got = kf[:, 2048:4096].rearrange("p (t k n) -> p t k n", t=TPC, k=TOP)

        PS = ctx.enter_context(nc.psum_tensor("PS", [P, 8 * CH], f32))

        def bank(b, n=1):
            return PS[:, b * CH:(b + n) * CH]

        s_pass = sem("s_pass")
        s_const = sem("s_const")
        s_x = [sem(f"s_x{i}") for i in range(4)]
        s_dve = sem("s_dve")
        s_var = sem("s_var")
        s_std = sem("s_std")
        s_xn = sem("s_xn")
        s_tr = sem("s_tr")
        s_xc = sem("s_xc")
        s_xg = sem("s_xg")
        s_qk = sem("s_qk")
        s_hi = sem("s_hi")
        s_sq = sem("s_sq")
        s_res = sem("s_res")
        s_p2 = sem("s_p2")
        s_p3 = sem("s_p3")
        s_store = sem("s_store")
        s_v = sem("s_v")
        s_vc = sem("s_vc")
        s_lg = sem("s_lg")
        s_rt = sem("s_rt")
        s_nr = sem("s_nr")
        s_nm = sem("s_nm")
        s_mk = sem("s_mk")
        s_bound = sem("s_bound")
        s_grow = sem("s_grow")
        s_gcol = sem("s_gcol")
        s_flag = sem("s_flag")
        s_gload = sem("s_gload")
        s_gs = sem("s_gs")
        s_gr = sem("s_gr")
        s_gneg = sem("s_gneg")
        s_gt = sem("s_gt")
        s_gc = sem("s_gc")
        s_loop = sem("s_loop")
        s_shift = sem("s_shift")
        s_sst = sem("s_sst")
        s_ones = sem("s_ones")
        s_stack = sem("s_stack")
        s_lg_e = sem("s_lg_e")
        s_lg_m = sem("s_lg_m")
        s_scores = sem("s_scores")
        s_exp = sem("s_exp")
        s_vh = sem("s_vh")
        s_pv = sem("s_pv")
        s_osb = sem("s_osb")
        s_red = sem("s_red")
        s_norm = sem("s_norm")
        s_loop_a = sem("s_loop_a")
        s_w = [sem("s_w0"), sem("s_w1")]
        s_ab = sem("s_ab")
        s_gin = sem("s_gin")
        s_prod = sem("s_prod")
        s_hid = sem("s_hid")
        s_y = sem("s_y")
        s_acc = sem("s_acc")
        s_one = sem("s_one")
        s_xst = sem("s_xst")
        s_nsq = sem("s_nsq")
        s_s1 = sem("s_s1")
        s_s2 = sem("s_s2")
        s_s3 = sem("s_s3")
        s_kroot = sem("s_kroot")
        s_kst = sem("s_kst")
        s_mask = sem("s_mask")
        s_pre = sem("s_pre")
        s_prc = sem("s_prc")
        s_zero = sem("s_zero")
        s_zst = sem("s_zst")
        s_pos = sem("s_pos")
        s_xin = sem("s_xin")
        s_idx = sem("s_idx")
        s_scat = sem("s_scat")
        s_xs = sem("s_xs")
        s_T = sem("s_T")
        s_xsT = sem("s_xsT")
        s_yc = sem("s_yc")
        s_yst = sem("s_yst")
        s_idg = sem("s_idg")
        s_got = sem("s_got")
        s_used = sem("s_used")
        s_hb = sem("s_hb")
        s_sum = sem("s_sum")
        s_kfill = sem("s_kfill")
        s_gst = sem("s_gst")
        s_out = sem("s_out")

        x_v = x[0].rearrange("(a p) d -> p a d", p=P)
        out_v = out[0].rearrange("(a p) d -> p a d", p=P)
        store_v = qk_parts.rearrange("s (j p) t -> s p j t", p=P)
        N_CONST = 10

        block = ctx.enter_context(nc.Block())

        @block.sync
        def _(sp):
            for i in range(4):
                sp.dma_start(resid[:, 8 * i:8 * i + 8, :], x_v[:, 8 * i:8 * i + 8, :]).then_inc(s_x[i], 16)
            for w, src in enumerate((wqT, wkT, wvT)):
                sp.dma_start(wqkv[:, w, :, :], src.rearrange("(t p) n -> p t n", p=P)).then_inc(s_const, 16)
            sp.dma_start(ident_sb[:, :], ident).then_inc(s_const, 16)
            sp.dma_start(gT_sb[:, :, :], gT.rearrange("(t p) n -> p t n", p=P)).then_inc(s_const, 16)
            sp.dma_start(hones_sb[:, :, :], hones).then_inc(s_const, 16)
            sp.dma_start(gb_sb[:, :], gate_b.partition_broadcast(P)).then_inc(s_const, 16)
            sp.dma_start(prefix_sb[:, :], prefix).then_inc(s_const, 16)
            sp.dma_start(ones_sb[:, :], ones).then_inc(s_const, 16)
            sp.dma_start(steps_sb[:, :], steps_c.partition_broadcast(P)).then_inc(s_const, 16)
            with sp.Fori(0, NCH) as c:
                sp.wait_ge(s_xn, c + 1)
                sp.dma_start(xn_rows[ds(c * CH, CH), :].rearrange("(t p) d -> p t d", p=P), xn).then_inc(s_xst, 16)
                for s, ready in enumerate((s_hi, s_p2, s_p3)):
                    sp.wait_ge(ready, c * NJ + NJ)
                    sp.sem_inc(s_pass, 1)
                    sp.dma_start(store_v[s][:, :, ds(c * CH, CH)], part[:, s, :, :]).then_inc(s_store, 16)
                sp.wait_ge(s_s3, c + 1)
                sp.dma_start(qshift_parts[:, :, ds(c * CH, CH)].rearrange("s h t -> h s t"), spart).then_inc(s_sst, 16)

            def load_stack(h, half, done):
                for g, (a, b) in enumerate(PAIRS):
                    sp.dma_start(q_stack[g * HD:(g + 1) * HD, ds(half * T, T)],
                                 qk_parts[a, ds(h * HD, HD), :]).then_inc(done, 16)
                    sp.dma_start(k_stack[g * HD:(g + 1) * HD, ds(half * T, T)],
                                 qk_parts[b, ds(D + h * HD, HD), :]).then_inc(done, 16)

            def load_shift(h, half):
                sp.dma_start(q_stack[SROW:ROWS, ds(half * T, T)],
                             qshift_parts[:, ds(h, 1), :].rearrange("s h t -> (s h) t")).then_inc(s_stack, 16)
                sp.dma_start(k_stack[SROW:ROWS, ds(half * T, T)],
                             kshift[ds(h, 1), :].to_broadcast([NP_, T])).then_inc(s_stack, 16)

            sp.wait_ge(s_store, 16 * NP_ * NCH)
            sp.wait_ge(s_xst, 16 * NCH)
            sp.wait_ge(s_nr, NCH)
            sp.wait_ge(s_xg, NCH)
            load_stack(0, 0, s_stack)
            sp.wait_ge(s_flag, 1)
            flag = sp.value_load(flag_i[0:1, 0:1], min_val=0, max_val=1)
            with sp.If(flag):
                with sp.Fori(0, H) as h:
                    load_stack(h, 1, s_gload)
                    sp.wait_ge(s_gs, h * (2 * NT) + 2 * NT)
                    sp.sem_inc(s_pass, 1)
                for n in range(NCH):
                    sp.wait_ge(s_shift, n + 1)
                    sp.dma_start(qshift_parts[:, :, n * CH:(n + 1) * CH].rearrange("s h t -> h s t"), spart).then_inc(s_gst, 16)
                sp.wait_ge(s_gst, 16 * NCH)
            sp.wait_ge(s_sst, 16 * NCH)
            sp.wait_ge(s_mk, 2)
            sp.dma_start(kshift, kfill).then_inc(s_kst, 16)
            sp.wait_ge(s_kst, 16)
            load_shift(0, 0)
            sp.wait_ge(s_stack, 16 * STACK_DMAS)
            load_stack(1, 1, s_stack)
            load_shift(1, 1)
            sp.wait_ge(s_zero, 1)
            with sp.Fori(0, ST) as i:
                sp.dma_start(slot_x[ds(i * CH, CH), :].rearrange("(p a) d -> p (a d)", p=P), zeros).then_inc(s_zst, 16)
            sp.dma_start(xn_in[:, 0, :, :], xn_rows[0:CH, :].rearrange("(t p) d -> p t d", p=P)).then_inc(s_xin, 16)

            def load_head(h):
                sp.wait_ge(s_stack, h * (16 * STACK_DMAS))
                sp.wait_ge(s_scores, h * (4 * GI) - 4 * GI)
                sp.sem_inc(s_pass, 1)
                load_stack(h, h % 2, s_stack)
                load_shift(h, h % 2)

            with sp.Fori(2, NCH + 1) as h:
                load_head(h)
                sp.wait_ge(s_xin, h * 16 - 16)
                sp.dma_start(xn_in[:, ds((h - 1) % 2, 1), :, :].rearrange("p b t n -> p (b t) n"),
                             xn_rows[ds((h - 1) * CH, CH), :].rearrange("(t p) d -> p t d", p=P)).then_inc(s_xin, 16)
                sp.wait_ge(s_scat, (h - 1) * (16 * TPC * TOP))
                sp.sem_inc(s_pass, 1)
            with sp.Fori(NCH + 1, H) as h:
                load_head(h)

            def load_expert(slot, half):
                sp.dma_start(w13_sb[half][:, 0, :, :],
                             w1[ds(slot, 1), :, :].rearrange("e (t p) n -> p (e t) n", p=P)).then_inc(s_w[half], 16)
                sp.dma_start(w13_sb[half][:, 1, :, :],
                             w3[ds(slot, 1), :, :].rearrange("e (t p) n -> p (e t) n", p=P)).then_inc(s_w[half], 16)
                sp.dma_start(bias_sb[:, half, :], b13[ds(slot, 1), :, :].rearrange("e p n -> (e p) n")).then_inc(s_w[half], 16)
                sp.dma_start(w2_sb[half][:, 0:2, :],
                             w2[ds(slot, 1), 0:2 * P, :].rearrange("e (t p) n -> p (e t) n", p=P)).then_inc(s_w[half], 16)
                sp.dma_start(w2_sb[half][0:FT[2], 2, :],
                             w2[ds(slot, 1), 2 * P:F, :].rearrange("e p n -> (e p) n")).then_inc(s_w[half], 16)
                sp.dma_start(w2_sb[half][FT[2]:FT[2] + 1, 2, :], b2[ds(slot, 1), :]).then_inc(s_w[half], 16)

            def load_tile(m, half):
                slot = sp.value_load(tile_slot[0:1, ds(m, 1)], min_val=1, max_val=E)
                load_expert(slot, half)

            def store_y(m, half):
                sp.wait_ge(s_yc, m + 1)
                sp.sem_inc(s_pass, 1)
                sp.dma_start(slot_y[ds(m * CH, CH), :].rearrange("(t p) d -> p t d", p=P), y_sb[:, half, :, :]).then_inc(s_yst, 16)

            sp.wait_ge(s_pv, H * NCH)
            sp.wait_ge(s_pos, 2)
            load_tile(0, 0)
            load_tile(1, 1)
            with sp.Fori(0, (ST - 3) // 2) as p:
                for k in range(2):
                    store_y(p * 2 + k, k)
                    load_tile(p * 2 + (k + 2), k)
            store_y(ST - 3, 0)
            load_tile(ST - 1, 0)
            store_y(ST - 2, 1)
            load_expert(0, 1)
            store_y(ST - 1, 0)
            for c in range(NCH):
                sp.wait_ge(s_used, c + 1)
                sp.dma_start(out_v[:, c * TPC:(c + 1) * TPC, :], resid[:, c * TPC:(c + 1) * TPC, :]).then_inc(s_out, 16)
            sp.wait_ge(s_out, 16 * NCH)

        @block.tensor
        def _(pe):
            pe.wait_ge(s_const, 16 * N_CONST)

            def turn_xn(c):
                pe.wait_ge(s_xn, c + 1)
                for dt in range(DT):
                    for t in range(TPC):
                        last = pe.transpose(bank(dt)[:, t * P:(t + 1) * P], xn[:, t, dt * P:(dt + 1) * P], ident_sb[:, :])
                last.then_inc(s_tr, 1)

            def project(c, last_chunk=False):
                pe.wait_ge(s_xc, c + 1)
                for j in range(NJ):
                    if j >= 2:
                        pe.wait_ge(s_res, c * NJ + (j - 1))
                    for dt in range(DT):
                        last = pe.matmul(bank(2 + j % 2), wqkv[:, j // DT, dt, (j % DT) * P:(j % DT + 1) * P], xc[:, dt, :],
                                         start=(dt == 0), stop=(dt == DT - 1))
                    last.then_inc(s_qk, 1)
                for t in range(TPC):
                    for dt in range(DT):
                        last = pe.matmul(bank(4 + t // 2)[:, (t % 2) * D:(t % 2 + 1) * D], xc[:, dt, t * P:(t + 1) * P],
                                         wqkv[:, 2, dt, :], start=(dt == 0), stop=(dt == DT - 1))
                    if t % 2:
                        last.then_inc(s_v, 1)
                for t in range(TPC):
                    for dt in range(DT):
                        last = pe.matmul(bank(6)[:, t * E:(t + 1) * E], xc[:, dt, t * P:(t + 1) * P], gT_sb[:, dt, :],
                                         start=(dt == 0), stop=(dt == DT - 1))
                last.then_inc(s_lg, 1)
                if not last_chunk:
                    turn_xn(c + 1)
                pe.wait_ge(s_sq, c * NJ + NJ)
                for w in range(2):
                    for dt in range(DT):
                        last = pe.matmul(bank(7)[32 * w:32 * w + H, :], hones_b[:, dt, :], sq[:, w * DT + dt, :],
                                         start=(dt == 0), stop=(dt == DT - 1))
                last.then_inc(s_nr, 1)
                if not last_chunk:
                    pe.wait_ge(s_res, c * NJ + NJ)
                    pe.wait_ge(s_vc, c * 2 + 2)
                    pe.wait_ge(s_rt, c + 1)
                    pe.sem_inc(s_pass, 1)

            turn_xn(0)
            pe.wait_ge(s_hb, 1)
            project(0)
            with pe.Fori(1, NCH - 1) as c:
                pe.wait_ge(s_nm, c)
                pe.sem_inc(s_pass, 1)
                project(c)
            pe.wait_ge(s_nm, NCH - 1)
            project(NCH - 1, last_chunk=True)
            pe.wait_ge(s_gcol, 1)
            pe.transpose(bank(0)[0:1, 0:H], qmax[:, NCH + 1:NCH + 2], ident_sb[0:H, 0:H]).then_inc(s_grow, 1)
            pe.wait_ge(s_flag, 1)
            flag = pe.value_load(flag_i[0:1, 0:1], min_val=0, max_val=1)
            with pe.If(flag):
                with pe.Fori(0, H) as h:
                    pe.wait_ge(s_gload, h * (32 * len(PAIRS)) + 32 * len(PAIRS))
                    pe.sem_inc(s_pass, 1)
                    with pe.Fori(0, NT) as t:
                        for half in range(2):
                            for n in range(4):
                                col = T + (4 * half + n) * CH
                                last = pe.matmul(bank(4 * half + n), q_stack[0:SROW, ds(t * P + T, P)], k_stack[0:SROW, col:col + CH],
                                                 start=True, stop=True)
                            last.then_inc(s_gs, 1)
                        pe.wait_ge(s_gr, h * (2 * NT) + t * 2 + 2)
                        pe.sem_inc(s_pass, 1)
                pe.wait_ge(s_gneg, 1)
                pe.wait_ge(s_loop, H * NT)
                for t in range(NT):
                    last = pe.transpose(PS[0:H, t * P:(t + 1) * P], nmax[:, t, :], ident_sb[:, :])
                last.then_inc(s_gt, 1)

            def scores(it, g):
                c, lo = g // NG, (g % NG) * GK
                qcol = (it * (2 * CH) + c * CH) % (2 * T)
                kcol = (it // (NCH // 2)) % 2 * T
                for n, kt in enumerate(range(lo, lo + GK)):
                    last = pe.matmul(bank(GK * score_buffer(g) + n), k_stack[0:ROWS, ds(kcol + kt * P, P)],
                                     q_stack[0:ROWS, ds(qcol, CH)], start=True, stop=True)
                last.then_inc(s_scores, 1)

            def values(c, b):
                for j in range(4):
                    kt = 4 * b + j
                    slot = SLOT[c * NG + kt // GK]
                    last = pe.matmul(bank(6 + c)[VW * j:VW * (j + 1), :], v_head[:, c, kt, :],
                                     probs[:, slot, (kt % GK) * CH:(kt % GK + 1) * CH], start=(b == 0), stop=(b == NB - 1))
                if b == NB - 1:
                    last.then_inc(s_pv, 1)

            def reduce(c, n):
                pe.wait_ge(s_osb, n + 1)
                for t in range(TPC):
                    last = pe.transpose(bank(6 + c)[:, t * P:(t + 1) * P], o_sb[:, c, t * P:(t + 1) * P], ident_sb[:, :])
                last.then_inc(s_red, 1)

            def iteration(it, first, last):
                for g in range(GI):
                    c, gg = g // NG, g % NG
                    n = it * 2 + c
                    pe.wait_ge(s_exp, it * GI + g + 1)
                    for ahead in AFTER[g]:
                        if ahead < GI:
                            scores(it, ahead)
                        elif not last:
                            if ahead == GI:
                                pe.wait_ge(s_stack, ((it + 1) // (NCH // 2)) * (16 * STACK_DMAS) + 16 * STACK_DMAS)
                            scores(it + 1, ahead - GI)
                    for b in range(NB):
                        if (4 * b + 3) // GK == gg:
                            if b == 0:
                                pe.wait_ge(s_vh, n + 1)
                                if not first:
                                    pe.wait_ge(s_norm, n - 1)
                            values(c, b)
                    if gg == 4 and not (first and c == 0):
                        reduce(1 - c, n - 1)
                    if first and c == 1 and gg == NG - 2:
                        pe.wait_ge(s_mask, 1)
                        pe.wait_ge(s_norm, 1)
                        cm = chosen[:, :, :].rearrange("p t e -> p (t e)")
                        pe.matmul(bank(6)[:, 0:NT * E], prefix_sb[:, :], cm, start=True, stop=True)
                        pe.matmul(bank(6)[:, NT * E:2 * NT * E], ones_sb[:, :], cm, start=True, stop=True).then_inc(s_pre, 1)

            pe.wait_ge(s_stack, 16 * STACK_DMAS)
            for g in range(SB):
                scores(0, g)
            iteration(0, True, False)
            pe.wait_ge(s_prc, 1)
            with pe.Fori(1, ITERS - 1) as it:
                iteration(it, False, False)
            iteration(ITERS - 1, False, True)
            reduce(1, H * NCH - 1)

            def turn(m, half):
                pe.wait_ge(s_xs, m * 16 + 16)
                for dt in range(DT):
                    for t in range(TPC):
                        last = pe.transpose(bank(4 + dt)[:, t * P:(t + 1) * P], slot_in[:, half, t, dt * P:(dt + 1) * P], ident_sb[:, :])
                last.then_inc(s_T, 1)

            def up(half, j, tokens):
                for w in range(2):
                    for dt in range(DT):
                        last = pe.matmul(bank(2 * w + j % 2)[0:FT[j], :], w13_sb[half][:, w, dt, j * P:j * P + FT[j]],
                                         tokens(dt), start=(dt == 0), stop=(dt == DT - 1))
                last.then_inc(s_ab, 1)

            def down(half, m):
                pe.wait_ge(s_hid, m * 3 + 3)
                if not (isinstance(m, int) and m == 0):
                    pe.wait_ge(s_yc, m)
                for t in range(TPC):
                    for j in range(3):
                        rows = FT[j] + (j == 2)
                        last = pe.matmul(bank(6 + t // 2)[:, (t % 2) * D:(t % 2 + 1) * D], hid[0:rows, j, t * P:(t + 1) * P],
                                         w2_sb[half][0:rows, j, :], start=(j == 0), stop=(j == 2))
                last.then_inc(s_y, 1)

            def tile(m, half, half_before, tokens, first=False):
                if not first:
                    pe.wait_ge(s_prod, m * 3)
                up(half, 0, tokens)
                if not first:
                    down(half_before, m - 1)
                up(half, 1, tokens)
                pe.wait_ge(s_prod, m * 3 + 1)
                up(half, 2, tokens)

            def slots_tile(m, half, first=False, last=False):
                pe.wait_ge(s_xsT, m + 1)
                if not last:
                    turn(m + 1, 1 - half)
                pe.wait_ge(s_w[half], (m // 2) * (16 * WDMAS) + 16 * WDMAS)
                tile(m, half, 1 - half, lambda dt: slot_T[:, half, dt, :], first)

            def shared_tile(c, half_before):
                tile(c + ST, ST % 2, half_before, lambda dt: xnT[:, dt, ds(c * CH, CH)])

            pe.wait_ge(s_norm, H * NCH)
            pe.wait_ge(s_one, 1)
            turn(0, 0)
            slots_tile(0, 0, first=True)
            with pe.Fori(0, (ST - 3) // 2) as p:
                slots_tile(p * 2 + 1, 1)
                slots_tile(p * 2 + 2, 0)
            slots_tile(ST - 2, 1)
            slots_tile(ST - 1, 0, last=True)
            pe.wait_ge(s_w[1], (ST // 2 + 1) * (16 * WDMAS))
            shared_tile(0, 0)
            with pe.Fori(1, NCH) as c:
                shared_tile(c, 1)
            down(1, ST + NCH - 1)

        @block.scalar
        def _(act):
            act.wait_ge(s_var, 1)
            nc.scalar.activation(ln_t[:, 1, :], ln_t[:, 0, :], ACT.Sqrt).then_inc(s_std, 1)

            def take_xn(c):
                act.wait_ge(s_tr, c + 1)
                nc.scalar.activation(xc[:, 0, :], bank(0), ACT.Copy)
                nc.scalar.activation(xc[:, 1, :], bank(1), ACT.Copy).then_inc(s_xc, 1)

            def split(c, last_chunk=False):
                for j in range(NJ):
                    act.wait_ge(s_qk, c * NJ + (j + 1))
                    nc.scalar.activation(part[:, 0, j, :], bank(2 + j % 2), ACT.Copy).then_inc(s_hi, 1)
                    nc.scalar.activation(sq[:, j, :], bank(2 + j % 2), ACT.Square).then_inc(s_sq, 1)
                if not last_chunk:
                    act.wait_ge(s_xg, c + 1)
                    act.sem_inc(s_pass, 1)
                    take_xn(c + 1)
                act.wait_ge(s_nr, c + 1)
                nc.scalar.activation(qnorm, bank(7)[0:H, :], ACT.Sqrt).then_inc(s_nsq, 1)
                act.wait_ge(s_s3, c + 1)
                act.wait_ge(s_store, c * (16 * NP_) + 16 * NP_)
                act.sem_inc(s_pass, 1)

            take_xn(0)
            with act.Fori(0, NCH - 1) as c:
                split(c)
            split(NCH - 1, last_chunk=True)
            act.wait_ge(s_mk, 1)
            nc.scalar.activation(kmax[:, NCH + 1:NCH + 2], kmax[:, NCH:NCH + 1], ACT.Sqrt).then_inc(s_kroot, 1)
            def exps(it, first=False):
                for g in range(GI):
                    if first and g == 4:
                        act.wait_ge(s_lg_m, 1)
                        nc.scalar.activation(rt[:, 0, :, :], rt[:, 1, :, :], ACT.Exp).then_inc(s_lg_e, 1)
                    act.wait_ge(s_scores, it * GI + (g + 1))
                    nc.scalar.activation(probs[:, SLOT[g], :], bank(GK * score_buffer(g), GK), ACT.Exp,
                                         scale=ENERGY_SCALE).then_inc(s_exp, 1)

            exps(0, True)
            with act.Fori(1, ITERS) as it:
                exps(it)

            def hidden(m, half, first=False):
                for j in range(3):
                    act.wait_ge(s_ab, m * 3 + (j + 1))
                    if j == 2:
                        act.wait_ge(s_prod, m * 3 + 1)
                    elif not first:
                        act.wait_ge(s_prod, m * 3)
                    nc.scalar.activation(gate_in[0:FT[j], j % 2, :], bank(j % 2)[0:FT[j], :], ACT.Identity,
                                         bias=bias_sb[0:FT[j], half, j:j + 1]).then_inc(s_gin, 1)
                for j in range(3):
                    act.wait_ge(s_prod, m * 3 + (j + 1))
                    if j == 0 and not first:
                        act.wait_ge(s_y, m)
                    nc.scalar.activation(hid[0:FT[j], j, :], prod[0:FT[j], j % 2, :], ACT.Silu).then_inc(s_hid, 1)

            hidden(0, 0, first=True)
            with act.Fori(0, (ST - 1) // 2) as p:
                hidden(p * 2 + 1, 1)
                hidden(p * 2 + 2, 0)
            with act.Fori(ST, ST + NCH) as m:
                hidden(m, ST % 2)

        @block.gpsimd
        def _(pool):
            with pool.Fori(0, NCH) as c:
                pool.wait_ge(s_xc, c + 1)
                nc.gpsimd.tensor_copy(xnT[:, :, ds(c * CH, CH)], xc[:, :, :]).then_inc(s_xg, 1)
                for j in range(NJ):
                    pool.wait_ge(s_res, c * NJ + (j + 1))
                    pool.sem_inc(s_pass, 1)
                    nc.gpsimd.tensor_copy(part[:, 1, j, :], resd[:, j, :]).then_inc(s_p2, 1)
                    pool.wait_ge(s_p2, c * NJ + (j + 1))
                    nc.gpsimd.tensor_tensor(part[:, 2, j, :], resd[:, j, :], part[:, 1, j, :], ALU.subtract).then_inc(s_p3, 1)
                pool.wait_ge(s_s1, c * 2 + 2)
                pool.sem_inc(s_pass, 1)
                nc.gpsimd.tensor_copy(spart[:, 1, :], sres).then_inc(s_s2, 1)
                pool.wait_ge(s_s2, c + 1)
                nc.gpsimd.tensor_tensor(spart[:, 2, :], sres, spart[:, 1, :], ALU.subtract).then_inc(s_s3, 1)
                pool.wait_ge(s_store, c * (16 * NP_) + 16 * NP_)
                pool.wait_ge(s_sst, c * 16 + 16)
                pool.sem_inc(s_pass, 1)
            nc.gpsimd.memset(zeros, 0.0).then_inc(s_zero, 1)
            pool.wait_ge(s_zst, 16 * ST)
            pool.wait_ge(s_pos, 1)
            with pool.Fori(0, NCH // 2) as p:
                for b in range(2):
                    c = p * 2 + b
                    nc.gpsimd.tensor_copy(index_s[:, :, :], pos[:, ds(c * TPC, TPC), :]).then_inc(s_idx, 1)
                    pool.wait_ge(s_idx, c + 1)
                    pool.wait_ge(s_xin, c * 16 + 16)
                    pool.sem_inc(s_pass, 1)
                    for t in range(TPC):
                        for k in range(TOP):
                            nc.gpsimd.indirect_dma_start(
                                out=slot_x, out_offset=bass.IndirectOffsetOnAxis(ap=index_s[:, t, k:k + 1], axis=0),
                                in_=xn_in[:, b, t, :], in_offset=None).then_inc(s_scat, 16)
                    pool.wait_ge(s_scat, c * (16 * TPC * TOP) + 16 * TPC * TOP)
                    pool.sem_inc(s_pass, 1)

            def load_slots(m, half):
                nc.gpsimd.dma_start(slot_in[:, half, :, :],
                                    slot_x[ds(m * CH, CH), :].rearrange("(t p) d -> p t d", p=P)).then_inc(s_xs, 16)

            pool.wait_ge(s_scores, ITERS * GI)
            load_slots(0, 0)
            pool.wait_ge(s_xs, 16)
            load_slots(1, 1)

            def next_slots(m, half):
                pool.wait_ge(s_T, m - 1)
                pool.wait_ge(s_xs, m * 16)
                pool.sem_inc(s_pass, 1)
                load_slots(m, half)

            with pool.Fori(1, (ST - 1) // 2) as p:
                next_slots(p * 2, 0)
                next_slots(p * 2 + 1, 1)
            next_slots(ST - 1, 0)
            pool.wait_ge(s_yst, 16 * ST)
            with pool.Fori(0, NCH) as c:
                nc.gpsimd.tensor_copy(index_g[:, :, :], pos[:, ds(c * TPC, TPC), :]).then_inc(s_idg, 1)
                pool.wait_ge(s_idg, c + 1)
                pool.sem_inc(s_pass, 1)
                for t in range(TPC):
                    for k in range(TOP):
                        nc.gpsimd.indirect_dma_start(
                            out=got[:, t, k, :], out_offset=None,
                            in_=slot_y, in_offset=bass.IndirectOffsetOnAxis(ap=index_g[:, t, k:k + 1], axis=0)).then_inc(s_got, 16)
                pool.wait_ge(s_used, c + 1)
                pool.sem_inc(s_pass, 1)

        @block.vector
        def _(dve):
            steps = [0]

            def link(ins):
                steps[0] += 1
                ins.then_inc(s_dve, 1)
                dve.wait_ge(s_dve, steps[0])

            V = nc.vector
            V.memset(v_all[:, :, :], 1.0)
            for t in range(NT):
                if t % 8 == 0:
                    dve.wait_ge(s_x[t // 8], 16)
                last = V.bn_stats(stats[:, t, :], resid[:, t, :])
            link(last)
            for t in range(NT):
                last = V.bn_aggr(mv[:, t, :], stats[:, t, :])
            link(last)
            V.tensor_scalar(ln_t[:, 0, :], mv[:, :, 1], EPS, None, ALU.add).then_inc(s_var, 1)
            dve.wait_ge(s_var, 1)
            dve.wait_ge(s_std, 1)
            link(V.reciprocal(rstd[:, :], ln_t[:, 1, :]))
            link(V.tensor_tensor(ln_t[:, 2, :], rstd[:, :], rstd[:, :], ALU.mult))
            link(V.tensor_tensor(ln_t[:, 2, :], ln_t[:, 2, :], ln_t[:, 0, :], ALU.mult))
            link(V.tensor_scalar(ln_t[:, 2, :], ln_t[:, 2, :], -0.5, 1.5, ALU.mult, ALU.add))
            link(V.tensor_tensor(rstd[:, :], rstd[:, :], ln_t[:, 2, :], ALU.mult))

            dve.wait_ge(s_const, 16 * N_CONST)
            V.tensor_copy(hones_b[:, :, :], hones_sb[:, :, :]).then_inc(s_hb, 1)

            def normalise(c):
                for t in range(TPC):
                    last = V.tensor_scalar(xn[:, t, :], resid[:, ds(c * TPC + t, 1), :].rearrange("p a d -> p (a d)"),
                                           mv[:, ds(c * TPC + t, 1), 0], rstd[:, ds(c * TPC + t, 1)],
                                           ALU.subtract, ALU.mult)
                last.then_inc(s_xn, 1)

            def residuals(c, last_chunk=False):
                if not last_chunk:
                    dve.wait_ge(s_tr, c + 1)
                    dve.wait_ge(s_xst, c * 16 + 16)
                    dve.sem_inc(s_pass, 1)
                    normalise(c + 1)
                for j in range(NJ):
                    dve.wait_ge(s_sq, c * NJ + (j + 1))
                    V.tensor_tensor(resd[:, j, :], bank(2 + j % 2), part[:, 0, j, :], ALU.subtract).then_inc(s_res, 1)
                for b in range(2):
                    dve.wait_ge(s_v, c * 2 + (b + 1))
                    V.tensor_copy(v_all[:, ds(c * TPC + 2 * b, 2), 0:H * VC].rearrange("p t (h w) -> p t h w", w=VC)[:, :, :, 0:HD],
                                  bank(4 + b).rearrange("p (t h w) -> p t h w", t=2, w=HD)).then_inc(s_vc, 1)
                dve.wait_ge(s_lg, c + 1)
                V.tensor_copy(logits[:, ds(c * TPC, TPC), :], bank(6)[:, 0:TPC * E].rearrange("p (t e) -> p t e", t=TPC)).then_inc(s_rt, 1)
                dve.wait_ge(s_nsq, c + 1)
                V.reduce_max(kmax[:, ds(c, 1)], bank(7)[32:32 + H, :], axis=AX).then_inc(s_nm, 1)
                V.reduce_max(qmax[:, ds(c, 1)], qnorm, axis=AX)
                V.tensor_scalar(spart[:, 0, :], qnorm, -1.0, None, ALU.mult).then_inc(s_s1, 1)
                dve.wait_ge(s_s1, c * 2 + 1)
                V.scalar_tensor_tensor(sres, qnorm, -1.0, spart[:, 0, :], ALU.mult, ALU.subtract).then_inc(s_s1, 1)
                dve.wait_ge(s_p3, c * NJ + NJ)
                dve.wait_ge(s_sst, c * 16 + 16)
                dve.sem_inc(s_pass, 1)

            normalise(0)
            with dve.Fori(0, NCH - 1) as c:
                residuals(c)
            residuals(NCH - 1, last_chunk=True)
            dve.wait_ge(s_s1, 2 * NCH)
            link(V.reduce_max(qmax[:, NCH:NCH + 1], qmax[:, 0:NCH], axis=AX))
            V.reduce_max(kmax[:, NCH:NCH + 1], kmax[:, 0:NCH], axis=AX).then_inc(s_mk, 1)
            dve.wait_ge(s_kroot, 1)
            V.tensor_tensor(qmax[:, NCH + 1:NCH + 2], qmax[:, NCH:NCH + 1], kmax[:, NCH + 1:NCH + 2], ALU.mult).then_inc(s_gcol, 1)
            link(V.memset(kfill, 1.0))
            dve.wait_ge(s_grow, 1)
            link(V.reduce_max(flag_f[0:1, 0:1], bank(0)[0:1, 0:H], axis=AX))
            link(V.tensor_scalar(flag_f[0:1, 1:2], flag_f[0:1, 0:1], BOUND_LIMIT, None, ALU.is_le))
            link(V.tensor_scalar(flag_f[0:1, 2:3], flag_f[0:1, 1:2], -1.0, 1.0, ALU.mult, ALU.add))
            V.tensor_copy(flag_i[0:1, 0:1], flag_f[0:1, 2:3]).then_inc(s_flag, 1)
            dve.wait_ge(s_flag, 1)
            V.tensor_scalar(kfill, kfill, kmax[:, NCH + 1:NCH + 2], None, ALU.mult).then_inc(s_kfill, 1)
            dve.wait_ge(s_kfill, 1)
            flag = dve.value_load(flag_i[0:1, 0:1], min_val=0, max_val=1)
            with dve.If(flag):
                with dve.Fori(0, H) as h:
                    with dve.Fori(0, NT) as t:
                        for half in range(2):
                            dve.wait_ge(s_gs, h * (2 * NT) + t * 2 + (half + 1))
                            V.reduce_max(gmax[:, half:half + 1], bank(4 * half, 4), axis=AX).then_inc(s_gr, 1)
                        dve.wait_ge(s_gr, h * (2 * NT) + t * 2 + 2)
                        V.tensor_scalar(nmax[:, ds(t, 1), ds(h, 1)].rearrange("p a b -> p (a b)"), gmax[:, 0:1],
                                        gmax[:, 1:2], -1.0, ALU.max, ALU.mult).then_inc(s_loop, 1)
                        dve.wait_ge(s_loop, h * NT + t + 1)
                V.memset(kfill, 1.0).then_inc(s_gneg, 1)
                dve.wait_ge(s_gneg, 1)
                dve.wait_ge(s_gt, 1)
                for n in range(NCH):
                    if n:
                        dve.wait_ge(s_gst, 16 * n)
                    V.tensor_copy(spart[:, 0, :], PS[0:H, n * CH:(n + 1) * CH]).then_inc(s_gc, 1)
                    dve.wait_ge(s_gc, 3 * n + 1)
                    V.tensor_tensor(sres, PS[0:H, n * CH:(n + 1) * CH], spart[:, 0, :], ALU.subtract).then_inc(s_gc, 1)
                    dve.wait_ge(s_gc, 3 * n + 2)
                    V.tensor_copy(spart[:, 1, :], sres).then_inc(s_gc, 1)
                    dve.wait_ge(s_gc, 3 * n + 3)
                    V.tensor_tensor(spart[:, 2, :], sres, spart[:, 1, :], ALU.subtract).then_inc(s_shift, 1)
            V.engine_nop().then_inc(s_mk, 1)

            def copy_v(c, h):
                V.tensor_copy(v_head[:, c, :, :], v_all[:, :, ds(h * VC, VW)]).then_inc(s_vh, 1)

            copy_v(0, 0)
            copy_v(1, 0)

            def bc(ap):
                return ap.unsqueeze(2).to_broadcast([P, NT, E])

            def over_tokens(ap):
                return ap.unsqueeze(1).to_broadcast([P, NT, E])

            sc, bi, t1, oh1, oh2, at, cum = (rt[:, i, :, :] for i in range(7))
            lg = logits[:, :, :]
            down = over_tokens(steps_sb[:, 0:E])
            link(V.reduce_max(rs[:, 0, :], lg, axis=AX))
            V.tensor_tensor(bi, lg, bc(rs[:, 0, :]), ALU.subtract).then_inc(s_lg_m, 1)
            dve.wait_ge(s_lg_e, 1)
            link(V.reduce_sum(rs[:, 0, :], sc, axis=AX))
            link(V.reciprocal(rs[:, 1, :], rs[:, 0, :]))
            link(V.tensor_tensor(sc, sc, bc(rs[:, 1, :]), ALU.mult))
            link(V.tensor_tensor(bi, sc, over_tokens(gb_sb[:, :]), ALU.add))
            for k, oh in enumerate((oh1, oh2)):
                link(V.reduce_max(rs[:, 0, :], bi, axis=AX))
                link(V.tensor_tensor(t1, bi, bc(rs[:, 0, :]), ALU.is_equal))
                link(V.tensor_tensor(t1, t1, down, ALU.mult))
                link(V.reduce_max(rs[:, 1, :], t1, axis=AX))
                link(V.tensor_tensor(oh, down, bc(rs[:, 1, :]), ALU.is_equal))
                if k == 0:
                    link(V.scalar_tensor_tensor(bi, oh, -3.0e38, bi, ALU.mult, ALU.add))
            V.tensor_tensor(chosen[:, :, :], oh1, oh2, ALU.add).then_inc(s_mask, 1)
            for k, oh in enumerate((oh1, oh2)):
                link(V.tensor_tensor(t1, sc, oh, ALU.mult))
                link(V.reduce_sum(weight[:, :, k], t1, axis=AX))

            def places():
                cnt, nt, end, start = (sizes[:, i, :] for i in range(4))
                for e in range(E):
                    last = V.tensor_tensor_scan(cum[:, :, e], ones_sb[:, 0:NT], ranks[:, 1, :, e], 0.0, ALU.mult, ALU.add)
                link(last)
                link(V.tensor_copy(cnt, cum[:, NT - 1, :]))
                link(V.tensor_tensor(cmp_sz[:, :, :], cnt.unsqueeze(2).to_broadcast([P, E, E]),
                                     steps_sb[:, E:2 * E].unsqueeze(1).to_broadcast([P, E, E]), ALU.is_gt))
                link(V.reduce_sum(nt, cmp_sz[:, :, :], axis=AX))
                link(V.tensor_tensor_scan(end, ones_sb[:, 0:E], nt, 0.0, ALU.mult, ALU.add))
                link(V.tensor_tensor(start, end, nt, ALU.subtract))
                link(V.tensor_scalar(start, start, float(CH), None, ALU.mult))
                link(V.tensor_tensor(at, cum, ranks[:, 1, :, :], ALU.subtract))
                link(V.tensor_tensor(at, at, ranks[:, 0, :, :], ALU.add))
                link(V.tensor_tensor(at, at, over_tokens(start), ALU.add))
                for k, oh in enumerate((oh1, oh2)):
                    link(V.tensor_tensor(t1, at, oh, ALU.mult))
                    link(V.reduce_sum(posf[:, :, k], t1, axis=AX))
                V.tensor_copy(pos[:, :, :], posf[:, :, :]).then_inc(s_pos, 1)
                link(V.tensor_tensor(tile_c[:, :, :], steps_sb[0:1, 2 * E:2 * E + ST].unsqueeze(2).to_broadcast([1, ST, E]),
                                     end[0:1, :].unsqueeze(1).to_broadcast([1, ST, E]), ALU.is_ge))
                link(V.reduce_sum(tile_f[:, :], tile_c[:, :, :], axis=AX))
                link(V.tensor_scalar(tile_f[:, :], tile_f[:, :], float(E - 1), 1.0, ALU.min, ALU.add))
                V.tensor_copy(tile_slot[:, :], tile_f[:, :]).then_inc(s_pos, 1)

            def output(it, c):
                dve.wait_ge(s_pv, it * 2 + (c + 1))
                V.tensor_copy(o_sb[:, c, :], bank(6 + c)).then_inc(s_osb, 1)
                copy_v(c, ((it + 1) // (NCH // 2)) % H)
                dve.wait_ge(s_red, it * 2 + (c + 1))
                o = bank(6 + c).rearrange("p (t j w) -> p t w j", t=TPC, j=P // VW)[:, :, 0:VC, :]
                V.reduce_sum(o_n[:, c, :, :], o, axis=AX).then_inc(s_norm, 1)
                dve.wait_ge(s_norm, it * 2 + (c + 1))
                V.reciprocal(rec[:, c, :], o_n[:, c, :, HD]).then_inc(s_loop_a, 1)
                dve.wait_ge(s_loop_a, it * 6 + (3 * c + 1))
                V.tensor_tensor(o_n[:, c, :, 0:HD], o_n[:, c, :, 0:HD], rec[:, c, :].unsqueeze(2).to_broadcast([P, TPC, HD]),
                                ALU.mult).then_inc(s_loop_a, 1)
                dve.wait_ge(s_loop_a, it * 6 + (3 * c + 2))
                dst = resid[:, ds(((it % (NCH // 2)) * 2 + c) * TPC, TPC), ds((it // (NCH // 2)) * HD, HD)]
                V.tensor_tensor(dst, dst, o_n[:, c, :, 0:HD], ALU.add).then_inc(s_loop_a, 1)

            output(0, 0)
            dve.wait_ge(s_pre, 1)
            V.tensor_copy(ranks[:, :, :, :].rearrange("p a t e -> p (a t e)"), bank(6)).then_inc(s_prc, 1)
            dve.wait_ge(s_prc, 1)
            output(0, 1)
            places()
            with dve.Fori(1, ITERS) as it:
                for c in range(2):
                    output(it, c)
            dve.wait_ge(s_loop_a, ITERS * 6)

            dve.wait_ge(s_scat, 16 * NT * TOP)
            V.memset(hid[FT[2]:FT[2] + 1, 2, :], 1.0).then_inc(s_one, 1)
            dve.wait_ge(s_one, 1)

            def tokens_in(m, half):
                dve.wait_ge(s_T, m + 1)
                V.tensor_copy(slot_T[:, half, :, :].rearrange("p t n -> p (t n)"), bank(4, 2)).then_inc(s_xsT, 1)

            def product(m, half, j, first=False):
                dve.wait_ge(s_gin, m * 3 + (j + 1))
                if not first or j == 2:
                    dve.wait_ge(s_hid, m * 3 + (j - 1))
                V.scalar_tensor_tensor(prod[0:FT[j], j % 2, :], bank(2 + j % 2)[0:FT[j], :], bias_sb[0:FT[j], half, 3 + j:4 + j],
                                       gate_in[0:FT[j], j % 2, :], ALU.add, ALU.mult).then_inc(s_prod, 1)

            def keep(m, half, wait=True):
                dve.wait_ge(s_y, m + 1)
                if wait:
                    dve.wait_ge(s_yst, m * 16 - 16)
                V.tensor_copy(y_sb[:, half, :, :].rearrange("p t n -> p (t n)"), bank(6, 2)).then_inc(s_yc, 1)

            def add_shared(c):
                dve.wait_ge(s_y, c + (ST + 1))
                dst = resid[:, ds(c * TPC, TPC), :].rearrange("p t n -> p (t n)")
                V.tensor_tensor(dst, dst, bank(6, 2), ALU.add).then_inc(s_yc, 1)
                dve.wait_ge(s_yc, c + (ST + 1))

            def combine(c):
                dve.wait_ge(s_got, c * (16 * TPC * TOP) + 16 * TPC * TOP)
                for k in range(TOP):
                    for t in range(TPC):
                        row = resid[:, ds(c * TPC + t, 1), :].rearrange("p a d -> p (a d)")
                        last = V.scalar_tensor_tensor(row, got[:, t, k, :], weight[:, ds(c * TPC + t, 1), k], row, ALU.mult, ALU.add)
                    if k == 0:
                        last.then_inc(s_sum, 1)
                        dve.wait_ge(s_sum, c + 1)
                last.then_inc(s_used, 1)

            def slots_tile(m, half, last=False, wait=True):
                if not last:
                    tokens_in(m + 1, 1 - half)
                product(m, half, 0)
                keep(m - 1, 1 - half, wait)
                product(m, half, 1)
                product(m, half, 2)

            tokens_in(0, 0)
            tokens_in(1, 1)
            for j in range(3):
                product(0, 0, j, first=True)
            slots_tile(1, 1, wait=False)
            slots_tile(2, 0, wait=False)
            with dve.Fori(1, (ST - 3) // 2) as p:
                slots_tile(p * 2 + 1, 1)
                slots_tile(p * 2 + 2, 0)
            slots_tile(ST - 2, 1)
            slots_tile(ST - 1, 0, last=True)
            for c in range(NCH):
                product(c + ST, ST % 2, 0)
                if c == 0:
                    keep(ST - 1, 0)
                else:
                    add_shared(c - 1)
                product(c + ST, ST % 2, 1)
                product(c + ST, ST % 2, 2)
                if c >= 2:
                    combine(c - 2)
            combine(NCH - 2)
            add_shared(NCH - 1)
            combine(NCH - 1)


def kernel(**inputs):
    import numpy as np
    import concourse.bacc as bacc
    from concourse import mybir as mb
    from concourse.bass_utils import run_bass_kernel_spmd

    a = {k[3:]: np.ascontiguousarray(v) for k, v in inputs.items()}

    def columns(shared, routed):
        b = np.concatenate([shared[None], routed], 0)
        full = np.zeros((NS, 3 * P), b.dtype)
        full[:, :F] = b
        return full.reshape(NS, 3, P).transpose(0, 2, 1)

    def slots(shared, routed):
        return np.concatenate([shared[None], routed], 0)

    hones = np.zeros((P, DT, H), np.float32)
    for p in range(P):
        for t in range(DT):
            hones[p, t, t * (P // HD) + p // HD] = 1.0
    arrays = {
        "x": a["attn_x"], "wqT": np.ascontiguousarray(a["attn_Wq"].T), "wkT": np.ascontiguousarray(a["attn_Wk"].T),
        "wvT": np.ascontiguousarray(a["attn_Wv"].T), "gT": np.ascontiguousarray(a["ffn_gate_w"].T), "gate_b": a["ffn_gate_b"],
        "w1": slots(a["ffn_sw1"], a["ffn_w1"]), "w3": slots(a["ffn_sw3"], a["ffn_w3"]), "w2": slots(a["ffn_sw2"], a["ffn_w2"]),
        "b13": np.ascontiguousarray(np.concatenate([columns(a["ffn_sb1"], a["ffn_b1"]), columns(a["ffn_sb3"], a["ffn_b3"])], 2)),
        "b2": slots(a["ffn_sb2"], a["ffn_b2"]),
        "ident": np.eye(P, dtype=np.float32), "hones": hones,
        "prefix": np.triu(np.ones((P, P), np.float32), 1), "ones": np.ones((P, P), np.float32),
        "steps": np.concatenate([E - np.arange(E), CH * np.arange(E), np.arange(ST)]).astype(np.float32),
    }
    nc = bacc.Bacc("TRN2", target_bir_lowering=False, num_devices=1)
    aps = [nc.dram_tensor("in_" + n, v.shape, mb.dt.from_np(v.dtype), kind="ExternalInput").ap() for n, v in arrays.items()]
    out = nc.dram_tensor("out_0", (1, T, D), mb.dt.float32, kind="ExternalOutput").ap()
    layer_program(nc, *aps, out)
    r = run_bass_kernel_spmd(nc, [{"in_" + n: v for n, v in arrays.items()}], core_ids=[0])
    return r.results[0]["out_0"]
```

```python
import concourse.bass as bass
from concourse import mybir
from contextlib import ExitStack

T = 4096
D = 256
H = 16
HD = D // H
E = 8
NS = E + 1
F = 352
P = 128
EPS = 1e-5
NT = T // P
CH = 512
NCH = T // CH
TPC = CH // P
DT = D // P
NJ = 2 * DT
NP_ = 3
PAIRS = [(0, 0), (0, 1), (1, 0), (1, 1), (0, 2), (2, 0)]
SROW = HD * len(PAIRS)
ROWS = SROW + NP_
ENERGY_SCALE = 1.0 / 16.0
BOUND_LIMIT = 40.0 * 16.0
GK = 2
SB = 3
NG = -(-NT // GK)
GI = 2 * NG
NPB = 6
NB = NT // 4
ITERS = H * NCH // 2
VC = HD + 1
VW = 32
FT = [128, 128, 96]
STACK_DMAS = 2 * len(PAIRS) + 2
TOP = 2
ST = (TOP * T + E * (CH - 1)) // CH
WDMAS = 5
LN_FIRST = 8
X_LOADS = (0, 8, 16, 24, NT)
WHALF = 2 * DT * F + 3 * D


def slot_of_group():
    slots, left = [], GI
    while left:
        n = 6 if left % 5 else 5
        slots += list(range(n))
        left -= n
    return slots


SLOT = slot_of_group()


def score_buffer(g):
    return g % GI % SB


def made_after():
    after, step = [[] for _ in range(GI)], -1
    for g in range(SB, GI + SB):
        before = max(x for x in range(g) if score_buffer(x) == score_buffer(g))
        step = max(step, before)
        after[step].append(g)
    return after


AFTER = made_after()


def layer_program(nc, x, wqT, wkT, wvT, gT, gate_b, w1, w3, w2, b13, b2, ident, hones, prefix, ones, steps_c, out):
    f32 = mybir.dt.float32
    f32r = mybir.dt.float32r
    bf16 = mybir.dt.bfloat16
    i32 = mybir.dt.int32
    u32 = mybir.dt.uint32
    ALU = mybir.AluOpType
    ACT = mybir.ActivationFunctionType
    AX = mybir.AxisListType.X
    ds = bass.ds

    ctx = ExitStack()
    with ctx:
        def sb(name, shape, dt):
            return ctx.enter_context(nc.sbuf_tensor(name, shape, dt))

        def sem(name):
            return ctx.enter_context(nc.semaphore(name))

        qk_parts = nc.dram_tensor("qk_parts", (NP_, 2 * D, T), bf16, kind="Internal").ap()
        qshift_parts = nc.dram_tensor("qshift_parts", (NP_, H, T), bf16, kind="Internal").ap()
        kshift = nc.dram_tensor("kshift", (H, T), bf16, kind="Internal").ap()
        xn_rows = nc.dram_tensor("xn_rows", (T, D), f32, kind="Internal").ap()
        slot_x = nc.dram_tensor("slot_x", (ST * CH, D), f32, kind="Internal").ap()
        slot_y = nc.dram_tensor("slot_y", (ST * CH, D), f32, kind="Internal").ap()

        resid = sb("resid", [P, NT, D], f32)
        xnT = sb("xnT", [P, DT, T], f32)
        ident_sb = sb("ident_sb", [P, P], f32)
        hones_b = sb("hones_b", [P, DT, H], bf16)
        hones_sb = sb("hones_sb", [P, DT, H], f32)
        gT_sb = sb("gT_sb", [P, DT, E], f32)
        gb_sb = sb("gb_sb", [P, E], f32)
        prefix_sb = sb("prefix_sb", [P, P], f32)
        ones_sb = sb("ones_sb", [P, P], f32)
        steps_sb = sb("steps_sb", [P, 2 * E + ST], f32)
        bias_sb = sb("bias_sb", [P, 2, 6], f32)
        stats = sb("stats", [P, NT, 6], f32)
        mv = sb("mv", [P, NT, 2], f32)
        rstd = sb("rstd", [P, NT], f32)
        ln_t = sb("ln_t", [P, 3, NT], f32)
        logits = sb("logits", [P, NT, E], f32)
        rt = sb("rt", [P, 7, NT, E], f32)
        rs = sb("rs", [P, 3, NT], f32)
        sizes = sb("sizes", [P, 4, E], f32)
        cmp_sz = sb("cmp_sz", [P, E, E], f32)
        weight = sb("weight", [P, NT, TOP], f32)
        posf = sb("posf", [P, NT, TOP], f32)
        pos = sb("pos", [P, NT, TOP], u32)
        tile_c = sb("tile_c", [1, ST, E], f32)
        tile_f = sb("tile_f", [1, ST], f32)
        tile_slot = sb("tile_slot", [1, ST], i32)
        index_s = sb("index_s", [P, TPC, TOP], u32)
        index_g = sb("index_g", [P, 3, TPC, TOP], u32)
        rec = sb("rec", [P, 2, TPC], f32)
        o_n = sb("o_n", [P, 2, TPC, VC], f32)
        kmax = sb("kmax", [H, NCH + 3], f32)
        qmax = sb("qmax", [H, NCH + 2], f32)
        flag_f = sb("flag_f", [1, 4], f32)
        flag_i = sb("flag_i", [1, 1], i32)
        gmax = sb("gmax", [P, 2], f32)

        stage = ExitStack()
        with stage:
            def sa(name, shape, dt):
                return stage.enter_context(nc.sbuf_tensor(name, shape, dt))

            spare = sa("spare", [P, 2 * WHALF + TPC * D], f32)
            q_stack = sa("q_stack", [P, 2 * T], bf16)
            k_stack = sa("k_stack", [P, 2 * T], bf16)
            probs = sa("probs", [P, NPB, GK * CH], f32)
            v_all = sa("v_all", [P, NT, H * VC + VW - VC], f32)
            v_head = sa("v_head", [P, 2, NT, VW], f32)
            o_sb = sa("o_sb", [P, 2, CH], f32)
        w_raw = sb("w_raw", [P, 2, WHALF], f32)
        slot_in = sb("slot_in", [P, 2, TPC, D], f32)
        w_hi = sb("w_hi", [P, 2, WHALF], f32r)
        w_lo = sb("w_lo", [P, 2, WHALF], f32r)
        x_hi = sb("x_hi", [P, 2, DT * CH], f32r)
        x_lo = sb("x_lo", [P, 2, DT * CH], f32r)
        gate_in = sb("gate_in", [P, 2, CH], f32)
        prod = sb("prod", [P, 2, CH], f32)
        hid = sb("hid", [P, 2, CH], f32)
        hid_hi = sb("hid_hi", [P, 3, CH], f32r)
        hid_lo = sb("hid_lo", [P, 3, CH], f32r)
        y_sb = sb("y_sb", [P, 2, TPC, D], f32)
        got_sb = sb("got_sb", [P, TPC, TOP, D], f32)
        got = [buf[:, :, :, :].rearrange("p a t n -> p (a t n)").rearrange("p (t k n) -> p t k n", t=TPC, k=TOP)
               for buf in (got_sb, slot_in, y_sb)]

        qf = q_stack[:, :].bitcast(f32)
        kf = k_stack[:, :].bitcast(f32)
        xn = qf[:, 0:TPC * D].rearrange("p (t d) -> p t d", t=TPC)
        xc = qf[:, 1024:2048].rearrange("p (t n) -> p t n", t=DT)
        resd = qf[:, 2048:4096].rearrange("p (j n) -> p j n", j=NJ)
        sq = kf[:, 0:1024].bitcast(bf16).rearrange("p (j n) -> p j n", j=NJ)
        wqkv = kf[:, 2048:2048 + 3 * DT * D].rearrange("p (w t n) -> p w t n", w=3, t=DT)
        part = spare[:, 0:3072].bitcast(bf16).rearrange("p (s j n) -> p s j n", s=NP_, j=NJ)
        pflat = probs[:, :, :].rearrange("p a b -> p (a b)")
        kfill = pflat[0:H, 0:T // 2].bitcast(bf16)
        qnorm = pflat[0:H, 2048:2048 + CH]
        sres = pflat[0:H, 2560:2560 + CH]
        spart = pflat[0:H, 3072:3072 + 768].bitcast(bf16).rearrange("p (s n) -> p s n", s=NP_)
        xn_in = spare[:, 0:2048].rearrange("p (b t n) -> p b t n", b=2, t=TPC)
        zeros = spare[:, 2048:3072]
        nmax = spare[:, 3072:3584].rearrange("p (t h) -> p t h", t=NT)
        chosen = spare[:, 3584:3840].rearrange("p (t e) -> p t e", t=NT)
        ranks = spare[:, 3840:4352].rearrange("p (a t e) -> p a t e", a=2, t=NT)

        def w13(w, half):
            return w[:, half, 0:2 * DT * F].rearrange("p (w t n) -> p w t n", w=2, t=DT)

        def w2_of(w, half):
            return w[:, half, 2 * DT * F:WHALF].rearrange("p (t n) -> p t n", t=3)

        PS = ctx.enter_context(nc.psum_tensor("PS", [P, 8 * CH], f32))

        def bank(b, n=1):
            return PS[:, b * CH:(b + n) * CH]

        s_pass = sem("s_pass")
        s_const = sem("s_const")
        s_x = [sem(f"s_x{i}") for i in range(4)]
        s_dve = sem("s_dve")
        s_var = sem("s_var")
        s_std = sem("s_std")
        s_xn = sem("s_xn")
        s_tr = sem("s_tr")
        s_xc = sem("s_xc")
        s_xt = sem("s_xt")
        s_qk = sem("s_qk")
        s_hi = sem("s_hi")
        s_sq = sem("s_sq")
        s_res = sem("s_res")
        s_p2 = sem("s_p2")
        s_p3 = sem("s_p3")
        s_store = sem("s_store")
        s_v = sem("s_v")
        s_vc = sem("s_vc")
        s_lg = sem("s_lg")
        s_rt = sem("s_rt")
        s_nr = sem("s_nr")
        s_nm = sem("s_nm")
        s_mk = sem("s_mk")
        s_grow = sem("s_grow")
        s_gcol = sem("s_gcol")
        s_flag = sem("s_flag")
        s_gload = sem("s_gload")
        s_gs = sem("s_gs")
        s_gr = sem("s_gr")
        s_gneg = sem("s_gneg")
        s_gt = sem("s_gt")
        s_gc = sem("s_gc")
        s_loop = sem("s_loop")
        s_shift = sem("s_shift")
        s_sst = sem("s_sst")
        s_ones = sem("s_ones")
        s_stack = sem("s_stack")
        s_lg_e = sem("s_lg_e")
        s_lg_m = sem("s_lg_m")
        s_scores = sem("s_scores")
        s_exp = sem("s_exp")
        s_vh = sem("s_vh")
        s_pv = sem("s_pv")
        s_osb = sem("s_osb")
        s_red = sem("s_red")
        s_norm = sem("s_norm")
        s_loop_a = sem("s_loop_a")
        s_w = [sem("s_w0"), sem("s_w1")]
        s_b = [sem("s_b0"), sem("s_b1")]
        s_ab = sem("s_ab")
        s_gin = sem("s_gin")
        s_prod = sem("s_prod")
        s_hid = sem("s_hid")
        s_y = sem("s_y")
        s_one = sem("s_one")
        s_xst = sem("s_xst")
        s_nsq = sem("s_nsq")
        s_s1 = sem("s_s1")
        s_s2 = sem("s_s2")
        s_s3 = sem("s_s3")
        s_kroot = sem("s_kroot")
        s_kst = sem("s_kst")
        s_mask = sem("s_mask")
        s_pre = sem("s_pre")
        s_prc = sem("s_prc")
        s_zero = sem("s_zero")
        s_zst = sem("s_zst")
        s_pos = sem("s_pos")
        s_xin = sem("s_xin")
        s_idx = sem("s_idx")
        s_scat = sem("s_scat")
        s_xs = sem("s_xs")
        s_T = sem("s_T")
        s_yc = sem("s_yc")
        s_yst = [sem(f"s_yst{i}") for i in range(2)]
        s_idg = sem("s_idg")
        s_got = [sem(f"s_got{i}") for i in range(3)]
        s_used = sem("s_used")
        s_xboth = sem("s_xboth")
        s_wz = sem("s_wz")
        s_xhi = sem("s_xhi")
        s_w13h = sem("s_w13h")
        s_w13 = sem("s_w13")
        s_w2h = sem("s_w2h")
        s_w2 = sem("s_w2")
        s_hhi = sem("s_hhi")
        s_hlo = sem("s_hlo")
        s_hb = sem("s_hb")
        s_sum = sem("s_sum")
        s_kfill = sem("s_kfill")
        s_gst = sem("s_gst")
        s_out = sem("s_out")

        x_v = x[0].rearrange("(a p) d -> p a d", p=P)
        out_v = out[0].rearrange("(a p) d -> p a d", p=P)
        store_v = qk_parts.rearrange("s (j p) t -> s p j t", p=P)
        N_CONST = 10

        def up_bank(w, half, j):
            return bank(2 * w + (half + j) % 2)

        block = ctx.enter_context(nc.Block())

        @block.sync
        def _(sp):
            def load_x(i):
                lo, hi = X_LOADS[i], X_LOADS[i + 1]
                sp.dma_start(resid[:, lo:hi, :], x_v[:, lo:hi, :]).then_inc(s_x[i], 16)

            load_x(0)
            for w, src in enumerate((wqT, wkT, wvT)):
                sp.dma_start(wqkv[:, w, :, :], src.rearrange("(t p) n -> p t n", p=P)).then_inc(s_const, 16)
            sp.dma_start(ident_sb[:, :], ident).then_inc(s_const, 16)
            sp.dma_start(gT_sb[:, :, :], gT.rearrange("(t p) n -> p t n", p=P)).then_inc(s_const, 16)
            sp.dma_start(hones_sb[:, :, :], hones).then_inc(s_const, 16)
            sp.dma_start(gb_sb[:, :], gate_b.partition_broadcast(P)).then_inc(s_const, 16)
            sp.dma_start(prefix_sb[:, :], prefix).then_inc(s_const, 16)
            sp.dma_start(ones_sb[:, :], ones).then_inc(s_const, 16)
            sp.dma_start(steps_sb[:, :], steps_c.partition_broadcast(P)).then_inc(s_const, 16)
            for i in range(1, len(X_LOADS) - 1):
                load_x(i)
            with sp.Fori(0, NCH) as c:
                for s, ready in enumerate((s_hi, s_p2, s_p3)):
                    sp.wait_ge(ready, c * NJ + NJ)
                    sp.sem_inc(s_pass, 1)
                    sp.dma_start(store_v[s][:, :, ds(c * CH, CH)], part[:, s, :, :]).then_inc(s_store, 16)
                sp.wait_ge(s_s3, c + 1)
                sp.dma_start(qshift_parts[:, :, ds(c * CH, CH)].rearrange("s h t -> h s t"), spart).then_inc(s_sst, 16)

            def load_stack(h, half, done):
                for g, (a, b) in enumerate(PAIRS):
                    sp.dma_start(q_stack[g * HD:(g + 1) * HD, ds(half * T, T)],
                                 qk_parts[a, ds(h * HD, HD), :]).then_inc(done, 16)
                    sp.dma_start(k_stack[g * HD:(g + 1) * HD, ds(half * T, T)],
                                 qk_parts[b, ds(D + h * HD, HD), :]).then_inc(done, 16)

            def load_shift(h, half):
                sp.dma_start(q_stack[SROW:ROWS, ds(half * T, T)],
                             qshift_parts[:, ds(h, 1), :].rearrange("s h t -> (s h) t")).then_inc(s_stack, 16)
                sp.dma_start(k_stack[SROW:ROWS, ds(half * T, T)],
                             kshift[ds(h, 1), :].to_broadcast([NP_, T])).then_inc(s_stack, 16)

            sp.wait_ge(s_store, 16 * NP_ * NCH)
            sp.wait_ge(s_xst, 16 * NCH)
            sp.wait_ge(s_nr, NCH)
            sp.wait_ge(s_lg, NCH)
            load_stack(0, 0, s_stack)
            sp.wait_ge(s_flag, 1)
            flag = sp.value_load(flag_i[0:1, 0:1], min_val=0, max_val=1)
            with sp.If(flag):
                with sp.Fori(0, H) as h:
                    load_stack(h, 1, s_gload)
                    sp.wait_ge(s_gs, h * (2 * NT) + 2 * NT)
                    sp.sem_inc(s_pass, 1)
                for n in range(NCH):
                    sp.wait_ge(s_shift, n + 1)
                    sp.dma_start(qshift_parts[:, :, n * CH:(n + 1) * CH].rearrange("s h t -> h s t"), spart).then_inc(s_gst, 16)
                sp.wait_ge(s_gst, 16 * NCH)
            sp.wait_ge(s_sst, 16 * NCH)
            sp.wait_ge(s_mk, 2)
            sp.dma_start(kshift, kfill).then_inc(s_kst, 16)
            sp.wait_ge(s_kst, 16)
            load_shift(0, 0)
            sp.wait_ge(s_stack, 16 * STACK_DMAS)
            load_stack(1, 1, s_stack)
            load_shift(1, 1)
            sp.wait_ge(s_zero, 1)
            with sp.Fori(0, ST) as i:
                sp.dma_start(slot_x[ds(i * CH, CH), :].rearrange("(p a) d -> p (a d)", p=P), zeros).then_inc(s_zst, 16)
            sp.dma_start(xn_in[:, 0, :, :], xn_rows[0:CH, :].rearrange("(t p) d -> p t d", p=P)).then_inc(s_xin, 16)

            def load_head(h):
                sp.wait_ge(s_stack, h * (16 * STACK_DMAS))
                sp.wait_ge(s_scores, h * (4 * GI) - 4 * GI)
                sp.sem_inc(s_pass, 1)
                load_stack(h, h % 2, s_stack)
                load_shift(h, h % 2)

            with sp.Fori(2, NCH + 1) as h:
                load_head(h)
                sp.wait_ge(s_xin, h * 16 - 16)
                sp.dma_start(xn_in[:, ds((h - 1) % 2, 1), :, :].rearrange("p b t n -> p (b t) n"),
                             xn_rows[ds((h - 1) * CH, CH), :].rearrange("(t p) d -> p t d", p=P)).then_inc(s_xin, 16)
                sp.wait_ge(s_scat, (h - 1) * (16 * TPC * TOP))
                sp.sem_inc(s_pass, 1)
            with sp.Fori(NCH + 1, H) as h:
                load_head(h)

            def load_expert(slot, half):
                w13r, w2r = w13(w_raw, half), w2_of(w_raw, half)
                sp.dma_start(w13r[:, 0, :, :],
                             w1[ds(slot, 1), :, :].rearrange("e (t p) n -> p (e t) n", p=P)).then_inc(s_w[half], 16)
                sp.dma_start(w13r[:, 1, :, :],
                             w3[ds(slot, 1), :, :].rearrange("e (t p) n -> p (e t) n", p=P)).then_inc(s_w[half], 16)
                sp.dma_start(w2r[:, 0:2, :],
                             w2[ds(slot, 1), 0:2 * P, :].rearrange("e (t p) n -> p (e t) n", p=P)).then_inc(s_w[half], 16)
                sp.dma_start(w2r[0:FT[2], 2, :],
                             w2[ds(slot, 1), 2 * P:F, :].rearrange("e p n -> (e p) n")).then_inc(s_w[half], 16)
                sp.dma_start(w2r[FT[2]:FT[2] + 1, 2, :], b2[ds(slot, 1), :]).then_inc(s_w[half], 16)

            def load_biases(slot, half):
                sp.dma_start(bias_sb[:, half, :], b13[ds(slot, 1), :, :].rearrange("e p n -> (e p) n")).then_inc(s_b[half], 16)

            def expert_of(m):
                return sp.value_load(tile_slot[0:1, ds(m, 1)], min_val=1, max_val=E)

            def store_y(m, half):
                sp.wait_ge(s_yc, m + 1)
                sp.sem_inc(s_pass, 1)
                sp.dma_start(slot_y[ds(m * CH, CH), :].rearrange("(t p) d -> p t d", p=P), y_sb[:, half, :, :]).then_inc(s_yst[half], 16)

            def weights_split(m):
                sp.wait_ge(s_w2, m + 1)
                sp.sem_inc(s_pass, 1)

            def biases_used(m):
                sp.wait_ge(s_prod, m * 3 + 3)
                sp.sem_inc(s_pass, 1)

            sp.wait_ge(s_pos, 2)
            sp.wait_ge(s_wz, 1)
            for m in range(2):
                load_expert(expert_of(m), m)
                load_biases(expert_of(m), m)
            weights_split(0)
            load_expert(expert_of(2), 0)
            with sp.Fori(0, (ST - 3) // 2) as p:
                for k in range(2):
                    weights_split(p * 2 + (k + 1))
                    load_expert(expert_of(p * 2 + (k + 3)), 1 - k)
                    biases_used(p * 2 + k)
                    load_biases(expert_of(p * 2 + (k + 2)), k)
                    store_y(p * 2 + k, k)
            weights_split(ST - 2)
            load_expert(0, 1)
            biases_used(ST - 3)
            load_biases(expert_of(ST - 1), 0)
            store_y(ST - 3, 0)
            biases_used(ST - 2)
            load_biases(0, 1)
            store_y(ST - 2, 1)
            store_y(ST - 1, 0)
            for c in range(NCH):
                sp.wait_ge(s_used, c + 1)
                sp.wait_ge(s_yc, ST + c + 1)
                sp.sem_inc(s_pass, 1)
                sp.dma_start(out_v[:, c * TPC:(c + 1) * TPC, :], resid[:, c * TPC:(c + 1) * TPC, :]).then_inc(s_out, 16)
            sp.wait_ge(s_out, 16 * NCH)

        @block.tensor
        def _(pe):
            pe.wait_ge(s_const, 16 * N_CONST)

            def turn_xn(c):
                pe.wait_ge(s_xn, c + 1)
                for dt in range(DT):
                    for t in range(TPC):
                        last = pe.transpose(bank(dt)[:, t * P:(t + 1) * P], xn[:, t, dt * P:(dt + 1) * P], ident_sb[:, :])
                last.then_inc(s_tr, 1)

            def project(c, first_chunk=False, last_chunk=False):
                pe.wait_ge(s_xt, c + 1)
                if not first_chunk:
                    pe.wait_ge(s_res, c * NJ)
                pe.sem_inc(s_pass, 1)
                for j in range(NJ):
                    if j >= 2:
                        pe.wait_ge(s_res, c * NJ + (j - 1))
                    for dt in range(DT):
                        last = pe.matmul(bank(2 + j % 2), wqkv[:, j // DT, dt, (j % DT) * P:(j % DT + 1) * P],
                                         xnT[:, dt, ds(c * CH, CH)], start=(dt == 0), stop=(dt == DT - 1))
                    last.then_inc(s_qk, 1)
                if not last_chunk:
                    turn_xn(c + 1)
                pe.wait_ge(s_sq, c * NJ + NJ)
                if not first_chunk:
                    pe.wait_ge(s_nm, c)
                pe.sem_inc(s_pass, 1)
                for w in range(2):
                    for dt in range(DT):
                        last = pe.matmul(bank(7)[32 * w:32 * w + H, :], hones_b[:, dt, :], sq[:, w * DT + dt, :],
                                         start=(dt == 0), stop=(dt == DT - 1))
                last.then_inc(s_nr, 1)
                if not first_chunk:
                    pe.wait_ge(s_vc, c * 2)
                    pe.wait_ge(s_rt, c)
                pe.wait_ge(s_xc, c + 1)
                pe.sem_inc(s_pass, 1)
                for t in range(TPC):
                    for dt in range(DT):
                        last = pe.matmul(bank(4 + t // 2)[:, (t % 2) * D:(t % 2 + 1) * D], xc[:, dt, t * P:(t + 1) * P],
                                         wqkv[:, 2, dt, :], start=(dt == 0), stop=(dt == DT - 1))
                    if t % 2:
                        last.then_inc(s_v, 1)
                for t in range(TPC):
                    for dt in range(DT):
                        last = pe.matmul(bank(6)[:, t * E:(t + 1) * E], xc[:, dt, t * P:(t + 1) * P], gT_sb[:, dt, :],
                                         start=(dt == 0), stop=(dt == DT - 1))
                last.then_inc(s_lg, 1)

            turn_xn(0)
            pe.wait_ge(s_hb, 1)
            project(0, first_chunk=True)
            with pe.Fori(1, NCH - 1) as c:
                project(c)
            project(NCH - 1, last_chunk=True)
            pe.wait_ge(s_gcol, 1)
            pe.transpose(bank(0)[0:1, 0:H], qmax[:, NCH + 1:NCH + 2], ident_sb[0:H, 0:H]).then_inc(s_grow, 1)
            pe.wait_ge(s_flag, 1)
            flag = pe.value_load(flag_i[0:1, 0:1], min_val=0, max_val=1)
            with pe.If(flag):
                with pe.Fori(0, H) as h:
                    pe.wait_ge(s_gload, h * (32 * len(PAIRS)) + 32 * len(PAIRS))
                    pe.sem_inc(s_pass, 1)
                    with pe.Fori(0, NT) as t:
                        for half in range(2):
                            for n in range(4):
                                col = T + (4 * half + n) * CH
                                last = pe.matmul(bank(4 * half + n), q_stack[0:SROW, ds(t * P + T, P)], k_stack[0:SROW, col:col + CH],
                                                 start=True, stop=True)
                            last.then_inc(s_gs, 1)
                        pe.wait_ge(s_gr, h * (2 * NT) + t * 2 + 2)
                        pe.sem_inc(s_pass, 1)
                pe.wait_ge(s_gneg, 1)
                pe.wait_ge(s_loop, H * NT)
                for t in range(NT):
                    last = pe.transpose(PS[0:H, t * P:(t + 1) * P], nmax[:, t, :], ident_sb[:, :])
                last.then_inc(s_gt, 1)

            def scores(it, g):
                c, lo = g // NG, (g % NG) * GK
                qcol = (it * (2 * CH) + c * CH) % (2 * T)
                kcol = (it // (NCH // 2)) % 2 * T
                for n, kt in enumerate(range(lo, lo + GK)):
                    last = pe.matmul(bank(GK * score_buffer(g) + n), k_stack[0:ROWS, ds(kcol + kt * P, P)],
                                     q_stack[0:ROWS, ds(qcol, CH)], start=True, stop=True)
                last.then_inc(s_scores, 1)

            def values(c, b):
                for j in range(4):
                    kt = 4 * b + j
                    slot = SLOT[c * NG + kt // GK]
                    last = pe.matmul(bank(6 + c)[VW * j:VW * (j + 1), :], v_head[:, c, kt, :],
                                     probs[:, slot, (kt % GK) * CH:(kt % GK + 1) * CH], start=(b == 0), stop=(b == NB - 1))
                if b == NB - 1:
                    last.then_inc(s_pv, 1)

            def reduce(c, n):
                pe.wait_ge(s_osb, n + 1)
                for t in range(TPC):
                    last = pe.transpose(bank(6 + c)[:, t * P:(t + 1) * P], o_sb[:, c, t * P:(t + 1) * P], ident_sb[:, :])
                last.then_inc(s_red, 1)

            def iteration(it, first, last):
                for g in range(GI):
                    c, gg = g // NG, g % NG
                    n = it * 2 + c
                    pe.wait_ge(s_exp, it * GI + g + 1)
                    for ahead in AFTER[g]:
                        if ahead < GI:
                            scores(it, ahead)
                        elif not last:
                            if ahead == GI:
                                pe.wait_ge(s_stack, ((it + 1) // (NCH // 2)) * (16 * STACK_DMAS) + 16 * STACK_DMAS)
                            scores(it + 1, ahead - GI)
                    for b in range(NB):
                        if (4 * b + 3) // GK == gg:
                            if b == 0:
                                pe.wait_ge(s_vh, n + 1)
                                if not first:
                                    pe.wait_ge(s_norm, n - 1)
                            values(c, b)
                    if gg == 4 and not (first and c == 0):
                        reduce(1 - c, n - 1)
                    if first and c == 1 and gg == NG - 2:
                        pe.wait_ge(s_mask, 1)
                        pe.wait_ge(s_norm, 1)
                        cm = chosen[:, :, :].rearrange("p t e -> p (t e)")
                        pe.matmul(bank(6)[:, 0:NT * E], prefix_sb[:, :], cm, start=True, stop=True)
                        pe.matmul(bank(6)[:, NT * E:2 * NT * E], ones_sb[:, :], cm, start=True, stop=True).then_inc(s_pre, 1)

            pe.wait_ge(s_stack, 16 * STACK_DMAS)
            for g in range(SB):
                scores(0, g)
            iteration(0, True, False)
            pe.wait_ge(s_prc, 1)
            with pe.Fori(1, ITERS - 1) as it:
                iteration(it, False, False)
            iteration(ITERS - 1, False, True)
            reduce(1, H * NCH - 1)

            def turn(m, half):
                pe.wait_ge(s_xs, m * 16 + 16)
                for dt in range(DT):
                    for t in range(TPC):
                        last = pe.transpose(bank(4 + dt)[:, t * P:(t + 1) * P], slot_in[:, half, t, dt * P:(dt + 1) * P], ident_sb[:, :])
                last.then_inc(s_T, 1)

            def up(m, whalf, half, j):
                for w in range(2):
                    n = 0
                    for dt in range(DT):
                        for a, b in ((w_hi, x_hi), (w_hi, x_lo), (w_lo, x_hi)):
                            last = pe.matmul(up_bank(w, half, j)[0:FT[j], :], w13(a, whalf)[:, w, dt, j * P:j * P + FT[j]],
                                             b[:, half, dt * CH:(dt + 1) * CH], start=(n == 0), stop=(n == 3 * DT - 1))
                            n += 1
                last.then_inc(s_ab, 1)

            def down(m, whalf):
                pe.wait_ge(s_hlo, m * 3 + 3)
                if not (isinstance(m, int) and m == 0):
                    pe.wait_ge(s_yc, m)
                for t in range(TPC):
                    n = 0
                    for j in range(3):
                        rows = FT[j] + (j == 2)
                        for a, b in ((hid_hi, w_hi), (hid_hi, w_lo), (hid_lo, w_hi)):
                            last = pe.matmul(bank(6 + t // 2)[:, (t % 2) * D:(t % 2 + 1) * D], a[0:rows, j, t * P:(t + 1) * P],
                                             w2_of(b, whalf)[0:rows, j, :], start=(n == 0), stop=(n == 8))
                            n += 1
                last.then_inc(s_y, 1)

            def tile(m, whalf, half, whalf_before, first=False):
                pe.wait_ge(s_xboth, m + 1)
                if not first:
                    pe.wait_ge(s_prod, m * 3 - 1)
                up(m, whalf, half, 0)
                if not first:
                    pe.wait_ge(s_prod, m * 3)
                up(m, whalf, half, 1)
                if not first:
                    down(m - 1, whalf_before)
                pe.wait_ge(s_prod, m * 3 + 1)
                up(m, whalf, half, 2)

            def slots_tile(m, half, first=False, last=False):
                if not last:
                    pe.wait_ge(s_xboth, m + 1)
                    turn(m + 1, 1 - half)
                pe.wait_ge(s_w13, m + 1)
                if not first:
                    pe.wait_ge(s_w2, m)
                tile(m, half, half, 1 - half, first)

            SW = ST % 2
            turn(0, 0)
            pe.wait_ge(s_norm, H * NCH)
            pe.wait_ge(s_one, 1)
            slots_tile(0, 0, first=True)
            with pe.Fori(0, (ST - 3) // 2) as p:
                slots_tile(p * 2 + 1, 1)
                slots_tile(p * 2 + 2, 0)
            slots_tile(ST - 2, 1)
            slots_tile(ST - 1, 0, last=True)
            pe.wait_ge(s_w13, ST + 1)
            tile(ST, SW, SW, 1 - SW)
            pe.wait_ge(s_w2, ST + 1)
            with pe.Fori(0, (NCH - 2) // 2) as p:
                tile(p * 2 + (ST + 1), SW, 1 - SW, SW)
                tile(p * 2 + (ST + 2), SW, SW, SW)
            tile(ST + NCH - 1, SW, 1 - SW, SW)
            down(ST + NCH - 1, SW)

        @block.scalar
        def _(act):
            def root(part, lo, hi):
                act.wait_ge(s_var, part)
                nc.scalar.activation(ln_t[:, 1, lo:hi], ln_t[:, 0, lo:hi], ACT.Sqrt).then_inc(s_std, 1)

            def take_xn(c):
                act.wait_ge(s_tr, c + 1)
                if not (isinstance(c, int) and c == 0):
                    act.wait_ge(s_xst, c * 16)
                act.sem_inc(s_pass, 1)
                act.dma_start(xn_rows[ds(c * CH, CH), :].rearrange("(t p) d -> p t d", p=P), xn).then_inc(s_xst, 16)
                nc.scalar.activation(xnT[:, 0, ds(c * CH, CH)], bank(0), ACT.Copy)
                nc.scalar.activation(xnT[:, 1, ds(c * CH, CH)], bank(1), ACT.Copy).then_inc(s_xt, 1)

            def hold_xn(c, first=False):
                if not first:
                    act.wait_ge(s_lg, c)
                act.wait_ge(s_xt, c + 1)
                act.sem_inc(s_pass, 1)
                nc.scalar.activation(xc[:, :, :], xnT[:, :, ds(c * CH, CH)], ACT.Copy).then_inc(s_xc, 1)

            def split(c, first_chunk=False, last_chunk=False):
                if not first_chunk:
                    act.wait_ge(s_store, c * (16 * NP_))
                    act.sem_inc(s_pass, 1)

                def second(j):
                    act.wait_ge(s_res, c * NJ + (j + 1))
                    nc.scalar.activation(part[:, 1, j, :], resd[:, j, :], ACT.Copy).then_inc(s_p2, 1)

                for j in range(NJ):
                    act.wait_ge(s_qk, c * NJ + (j + 1))
                    nc.scalar.activation(part[:, 0, j, :], bank(2 + j % 2), ACT.Copy).then_inc(s_hi, 1)
                    nc.scalar.activation(sq[:, j, :], bank(2 + j % 2), ACT.Square).then_inc(s_sq, 1)
                    if j:
                        second(j - 1)
                if not last_chunk:
                    take_xn(c + 1)
                second(NJ - 1)
                act.wait_ge(s_nr, c + 1)
                if not first_chunk:
                    act.wait_ge(s_s1, c * 2)
                nc.scalar.activation(qnorm, bank(7)[0:H, :], ACT.Sqrt).then_inc(s_nsq, 1)
                if not last_chunk:
                    hold_xn(c + 1)

            root(1, 0, LN_FIRST)
            take_xn(0)
            hold_xn(0, first=True)
            root(2, LN_FIRST, NT)
            split(0, first_chunk=True)
            with act.Fori(1, NCH - 1) as c:
                split(c)
            split(NCH - 1, last_chunk=True)
            act.wait_ge(s_mk, 1)
            nc.scalar.activation(kmax[:, NCH + 1:NCH + 2], kmax[:, NCH:NCH + 1], ACT.Sqrt).then_inc(s_kroot, 1)
            def exps(it, first=False):
                for g in range(GI):
                    if first and g == 4:
                        act.wait_ge(s_lg_m, 1)
                        nc.scalar.activation(rt[:, 0, :, :], rt[:, 1, :, :], ACT.Exp).then_inc(s_lg_e, 1)
                    act.wait_ge(s_scores, it * GI + (g + 1))
                    nc.scalar.activation(probs[:, SLOT[g], :], bank(GK * score_buffer(g), GK), ACT.Exp,
                                         scale=ENERGY_SCALE).then_inc(s_exp, 1)

            exps(0, True)
            with act.Fori(1, ITERS) as it:
                exps(it)

            def tokens_hi(m, half, chunk=None):
                if chunk is None:
                    act.wait_ge(s_T, m + 1)
                    src, dst = bank(4, 2), x_hi[:, half, :]
                else:
                    act.wait_ge(s_ab, m * 3 - 3)
                    src, dst = xnT[:, :, ds(chunk * CH, CH)], x_hi[:, half, :].rearrange("p (t n) -> p t n", t=DT)
                nc.scalar.activation(dst, src, ACT.Copy).then_inc(s_xhi, 1)

            def weights13_hi(m, half):
                act.wait_ge(s_w[half], (m // 2) * (16 * WDMAS) + 16 * WDMAS)
                act.sem_inc(s_pass, 1)
                nc.scalar.activation(w_hi[:, half, 0:2 * DT * F], w_raw[:, half, 0:2 * DT * F], ACT.Copy).then_inc(s_w13h, 1)

            def weights2_hi(half):
                nc.scalar.activation(w_hi[:, half, 2 * DT * F:WHALF], w_raw[:, half, 2 * DT * F:WHALF], ACT.Copy).then_inc(s_w2h, 1)

            def gate(m, half, bhalf, j, shared):
                if j == 0:
                    act.wait_ge(s_b[bhalf], ((ST if shared else m) // 2) * 16 + 16)
                    act.sem_inc(s_pass, 1)
                act.wait_ge(s_ab, m * 3 + (j + 1))
                if j == 2:
                    act.wait_ge(s_prod, m * 3 + 1)
                elif not (isinstance(m, int) and m == 0):
                    act.wait_ge(s_prod, m * 3)
                nc.scalar.activation(gate_in[0:FT[j], j % 2, :], up_bank(0, half, j)[0:FT[j], :], ACT.Identity,
                                     bias=bias_sb[0:FT[j], bhalf, j:j + 1]).then_inc(s_gin, 1)

            def hidden(m, j, first=False):
                act.wait_ge(s_prod, m * 3 + (j + 1))
                if not first or j == 2:
                    act.wait_ge(s_hlo, m * 3 + (j - 1))
                nc.scalar.activation(hid[0:FT[j], j % 2, :], prod[0:FT[j], j % 2, :], ACT.Silu).then_inc(s_hid, 1)
                if not first and j == 0:
                    act.wait_ge(s_y, m)
                act.wait_ge(s_hid, m * 3 + (j + 1))
                nc.scalar.activation(hid_hi[0:FT[j], j, :], hid[0:FT[j], j % 2, :], ACT.Copy).then_inc(s_hhi, 1)

            def work(m, half, bhalf, chunk=None, tokens=True, weights=True, first=False, shared=False):
                if tokens:
                    tokens_hi(m + 1, 1 - half, chunk)
                if weights:
                    weights13_hi(m + 1, 1 - half)
                gate(m, half, bhalf, 0, shared)
                gate(m, half, bhalf, 1, shared)
                hidden(m, 0, first)
                if weights:
                    weights2_hi(1 - half)
                hidden(m, 1, first)
                gate(m, half, bhalf, 2, shared)
                hidden(m, 2, first)

            SW = ST % 2
            weights13_hi(0, 0)
            tokens_hi(0, 0)
            weights2_hi(0)
            work(0, 0, 0, first=True)
            with act.Fori(0, (ST - 3) // 2) as p:
                work(p * 2 + 1, 1, 1)
                work(p * 2 + 2, 0, 0)
            work(ST - 2, 1, 1)
            work(ST - 1, 0, 0, chunk=0)
            work(ST, SW, SW, chunk=1, weights=False, shared=True)
            with act.Fori(0, (NCH - 2) // 2) as p:
                work(p * 2 + (ST + 1), 1 - SW, SW, chunk=p * 2 + 2, weights=False, shared=True)
                work(p * 2 + (ST + 2), SW, SW, chunk=p * 2 + 3, weights=False, shared=True)
            work(ST + NCH - 1, 1 - SW, SW, tokens=False, weights=False, shared=True)

        @block.gpsimd
        def _(pool):
            nc.gpsimd.memset(v_all[:, :, :], 1.0)
            nc.gpsimd.memset(kfill, 1.0).then_inc(s_ones, 1)
            with pool.Fori(0, NCH) as c:
                for j in range(NJ):
                    pool.wait_ge(s_p2, c * NJ + (j + 1))
                    nc.gpsimd.tensor_tensor(part[:, 2, j, :], resd[:, j, :], part[:, 1, j, :], ALU.subtract).then_inc(s_p3, 1)
                pool.wait_ge(s_s1, c * 2 + 2)
                pool.sem_inc(s_pass, 1)
                nc.gpsimd.tensor_copy(spart[:, 1, :], sres).then_inc(s_s2, 1)
                pool.wait_ge(s_s2, c + 1)
                nc.gpsimd.tensor_tensor(spart[:, 2, :], sres, spart[:, 1, :], ALU.subtract).then_inc(s_s3, 1)
                pool.wait_ge(s_store, c * (16 * NP_) + 16 * NP_)
                pool.wait_ge(s_sst, c * 16 + 16)
                pool.sem_inc(s_pass, 1)
            nc.gpsimd.memset(zeros, 0.0).then_inc(s_zero, 1)
            pool.wait_ge(s_zst, 16 * ST)
            pool.wait_ge(s_pos, 1)
            with pool.Fori(0, NCH // 2) as p:
                for b in range(2):
                    c = p * 2 + b
                    nc.gpsimd.tensor_copy(index_s[:, :, :], pos[:, ds(c * TPC, TPC), :]).then_inc(s_idx, 1)
                    pool.wait_ge(s_idx, c + 1)
                    pool.wait_ge(s_xin, c * 16 + 16)
                    pool.sem_inc(s_pass, 1)
                    for t in range(TPC):
                        for k in range(TOP):
                            nc.gpsimd.indirect_dma_start(
                                out=slot_x, out_offset=bass.IndirectOffsetOnAxis(ap=index_s[:, t, k:k + 1], axis=0),
                                in_=xn_in[:, b, t, :], in_offset=None).then_inc(s_scat, 16)
                    pool.wait_ge(s_scat, c * (16 * TPC * TOP) + 16 * TPC * TOP)
                    pool.sem_inc(s_pass, 1)

            def load_slots(m, half):
                nc.gpsimd.dma_start(slot_in[:, half, :, :],
                                    slot_x[ds(m * CH, CH), :].rearrange("(t p) d -> p t d", p=P)).then_inc(s_xs, 16)

            pool.wait_ge(s_pos, 2)
            for half in range(2):
                last = nc.gpsimd.memset(w2_of(w_raw, half)[FT[2]:P, 2, :], 0.0)
            last.then_inc(s_wz, 1)
            load_slots(0, 0)
            pool.wait_ge(s_xs, 16)
            pool.wait_ge(s_scores, ITERS * GI)
            load_slots(1, 1)

            def next_slots(m, half):
                pool.wait_ge(s_T, m - 1)
                pool.wait_ge(s_xs, m * 16)
                pool.sem_inc(s_pass, 1)
                load_slots(m, half)

            with pool.Fori(1, (ST - 1) // 2) as p:
                next_slots(p * 2, 0)
                next_slots(p * 2 + 1, 1)
            next_slots(ST - 1, 0)
            pool.wait_ge(s_yst[0], 16 * ((ST + 1) // 2))
            pool.wait_ge(s_yst[1], 16 * (ST // 2))
            pool.wait_ge(s_T, ST)

            for c in range(NCH):
                b = c % 3
                if c >= 3:
                    pool.wait_ge(s_used, c - 2)
                nc.gpsimd.tensor_copy(index_g[:, b, :, :], pos[:, c * TPC:(c + 1) * TPC, :]).then_inc(s_idg, 1)
                pool.wait_ge(s_idg, c + 1)
                for t in range(TPC):
                    for k in range(TOP):
                        nc.gpsimd.indirect_dma_start(
                            out=got[b][:, t, k, :], out_offset=None, in_=slot_y,
                            in_offset=bass.IndirectOffsetOnAxis(ap=index_g[:, b, t, k:k + 1], axis=0)).then_inc(s_got[b], 16)

        @block.vector
        def _(dve):
            steps = [0]

            def link(ins):
                steps[0] += 1
                ins.then_inc(s_dve, 1)
                dve.wait_ge(s_dve, steps[0])

            V = nc.vector
            def layernorm_factors(part, lo, hi):
                for t in range(lo, hi):
                    if t in X_LOADS:
                        dve.wait_ge(s_x[X_LOADS.index(t)], 16)
                    last = V.bn_stats(stats[:, t, :], resid[:, t, :])
                link(last)
                for t in range(lo, hi):
                    last = V.bn_aggr(mv[:, t, :], stats[:, t, :])
                link(last)
                V.tensor_scalar(ln_t[:, 0, lo:hi], mv[:, lo:hi, 1], EPS, None, ALU.add).then_inc(s_var, 1)
                dve.wait_ge(s_var, part)
                dve.wait_ge(s_std, part)
                link(V.reciprocal(rstd[:, lo:hi], ln_t[:, 1, lo:hi]))
                link(V.tensor_tensor(ln_t[:, 2, lo:hi], rstd[:, lo:hi], rstd[:, lo:hi], ALU.mult))
                link(V.tensor_tensor(ln_t[:, 2, lo:hi], ln_t[:, 2, lo:hi], ln_t[:, 0, lo:hi], ALU.mult))
                link(V.tensor_scalar(ln_t[:, 2, lo:hi], ln_t[:, 2, lo:hi], -0.5, 1.5, ALU.mult, ALU.add))
                link(V.tensor_tensor(rstd[:, lo:hi], rstd[:, lo:hi], ln_t[:, 2, lo:hi], ALU.mult))

            def normalise(c):
                for t in range(TPC):
                    last = V.tensor_scalar(xn[:, t, :], resid[:, ds(c * TPC + t, 1), :].rearrange("p a d -> p (a d)"),
                                           mv[:, ds(c * TPC + t, 1), 0], rstd[:, ds(c * TPC + t, 1)],
                                           ALU.subtract, ALU.mult)
                last.then_inc(s_xn, 1)

            layernorm_factors(1, 0, LN_FIRST)
            normalise(0)
            dve.wait_ge(s_const, 16 * N_CONST)
            V.tensor_copy(hones_b[:, :, :], hones_sb[:, :, :]).then_inc(s_hb, 1)
            layernorm_factors(2, LN_FIRST, NT)
            dve.wait_ge(s_ones, 1)

            def residuals(c, first_chunk=False, last_chunk=False):
                if not first_chunk:
                    dve.wait_ge(s_p3, c * NJ)
                    dve.sem_inc(s_pass, 1)
                for j in range(NJ):
                    if j == 2 and not last_chunk:
                        dve.wait_ge(s_tr, c + 1)
                        dve.wait_ge(s_xst, c * 16 + 16)
                        dve.sem_inc(s_pass, 1)
                        normalise(c + 1)
                    dve.wait_ge(s_sq, c * NJ + (j + 1))
                    V.tensor_tensor(resd[:, j, :], bank(2 + j % 2), part[:, 0, j, :], ALU.subtract).then_inc(s_res, 1)
                dve.wait_ge(s_nsq, c + 1)
                V.reduce_max(kmax[:, ds(c, 1)], bank(7)[32:32 + H, :], axis=AX).then_inc(s_nm, 1)
                if not first_chunk:
                    dve.wait_ge(s_sst, c * 16)
                    dve.sem_inc(s_pass, 1)
                V.reduce_max(qmax[:, ds(c, 1)], qnorm, axis=AX)
                V.tensor_scalar(spart[:, 0, :], qnorm, -1.0, None, ALU.mult).then_inc(s_s1, 1)
                dve.wait_ge(s_s1, c * 2 + 1)
                V.scalar_tensor_tensor(sres, qnorm, -1.0, spart[:, 0, :], ALU.mult, ALU.subtract).then_inc(s_s1, 1)
                for b in range(2):
                    dve.wait_ge(s_v, c * 2 + (b + 1))
                    V.tensor_copy(v_all[:, ds(c * TPC + 2 * b, 2), 0:H * VC].rearrange("p t (h w) -> p t h w", w=VC)[:, :, :, 0:HD],
                                  bank(4 + b).rearrange("p (t h w) -> p t h w", t=2, w=HD)).then_inc(s_vc, 1)
                dve.wait_ge(s_lg, c + 1)
                V.tensor_copy(logits[:, ds(c * TPC, TPC), :], bank(6)[:, 0:TPC * E].rearrange("p (t e) -> p t e", t=TPC)).then_inc(s_rt, 1)

            residuals(0, first_chunk=True)
            with dve.Fori(1, NCH - 1) as c:
                residuals(c)
            residuals(NCH - 1, last_chunk=True)
            dve.wait_ge(s_nm, NCH)
            dve.wait_ge(s_s1, 2 * NCH)
            link(V.reduce_max(qmax[:, NCH:NCH + 1], qmax[:, 0:NCH], axis=AX))
            V.reduce_max(kmax[:, NCH:NCH + 1], kmax[:, 0:NCH], axis=AX).then_inc(s_mk, 1)
            dve.wait_ge(s_kroot, 1)
            V.tensor_tensor(qmax[:, NCH + 1:NCH + 2], qmax[:, NCH:NCH + 1], kmax[:, NCH + 1:NCH + 2], ALU.mult).then_inc(s_gcol, 1)
            dve.wait_ge(s_grow, 1)
            link(V.reduce_max(flag_f[0:1, 0:1], bank(0)[0:1, 0:H], axis=AX))
            link(V.tensor_scalar(flag_f[0:1, 1:2], flag_f[0:1, 0:1], BOUND_LIMIT, None, ALU.is_le))
            link(V.tensor_scalar(flag_f[0:1, 2:3], flag_f[0:1, 1:2], -1.0, 1.0, ALU.mult, ALU.add))
            V.tensor_copy(flag_i[0:1, 0:1], flag_f[0:1, 2:3]).then_inc(s_flag, 1)
            dve.wait_ge(s_flag, 1)
            V.tensor_scalar(kfill, kfill, kmax[:, NCH + 1:NCH + 2], None, ALU.mult).then_inc(s_kfill, 1)
            dve.wait_ge(s_kfill, 1)
            flag = dve.value_load(flag_i[0:1, 0:1], min_val=0, max_val=1)
            with dve.If(flag):
                with dve.Fori(0, H) as h:
                    with dve.Fori(0, NT) as t:
                        for half in range(2):
                            dve.wait_ge(s_gs, h * (2 * NT) + t * 2 + (half + 1))
                            V.reduce_max(gmax[:, half:half + 1], bank(4 * half, 4), axis=AX).then_inc(s_gr, 1)
                        dve.wait_ge(s_gr, h * (2 * NT) + t * 2 + 2)
                        V.tensor_scalar(nmax[:, ds(t, 1), ds(h, 1)].rearrange("p a b -> p (a b)"), gmax[:, 0:1],
                                        gmax[:, 1:2], -1.0, ALU.max, ALU.mult).then_inc(s_loop, 1)
                        dve.wait_ge(s_loop, h * NT + t + 1)
                V.memset(kfill, 1.0).then_inc(s_gneg, 1)
                dve.wait_ge(s_gneg, 1)
                dve.wait_ge(s_gt, 1)
                for n in range(NCH):
                    if n:
                        dve.wait_ge(s_gst, 16 * n)
                    V.tensor_copy(spart[:, 0, :], PS[0:H, n * CH:(n + 1) * CH]).then_inc(s_gc, 1)
                    dve.wait_ge(s_gc, 3 * n + 1)
                    V.tensor_tensor(sres, PS[0:H, n * CH:(n + 1) * CH], spart[:, 0, :], ALU.subtract).then_inc(s_gc, 1)
                    dve.wait_ge(s_gc, 3 * n + 2)
                    V.tensor_copy(spart[:, 1, :], sres).then_inc(s_gc, 1)
                    dve.wait_ge(s_gc, 3 * n + 3)
                    V.tensor_tensor(spart[:, 2, :], sres, spart[:, 1, :], ALU.subtract).then_inc(s_shift, 1)
            V.engine_nop().then_inc(s_mk, 1)

            def copy_v(c, h):
                V.tensor_copy(v_head[:, c, :, :], v_all[:, :, ds(h * VC, VW)]).then_inc(s_vh, 1)

            copy_v(0, 0)
            copy_v(1, 0)

            def bc(ap):
                return ap.unsqueeze(2).to_broadcast([P, NT, E])

            def over_tokens(ap):
                return ap.unsqueeze(1).to_broadcast([P, NT, E])

            sc, bi, t1, oh1, oh2, at, cum = (rt[:, i, :, :] for i in range(7))
            lg = logits[:, :, :]
            down = over_tokens(steps_sb[:, 0:E])
            link(V.reduce_max(rs[:, 0, :], lg, axis=AX))
            V.tensor_tensor(bi, lg, bc(rs[:, 0, :]), ALU.subtract).then_inc(s_lg_m, 1)
            dve.wait_ge(s_lg_e, 1)
            link(V.reduce_sum(rs[:, 0, :], sc, axis=AX))
            link(V.reciprocal(rs[:, 1, :], rs[:, 0, :]))
            link(V.tensor_tensor(sc, sc, bc(rs[:, 1, :]), ALU.mult))
            link(V.tensor_tensor(bi, sc, over_tokens(gb_sb[:, :]), ALU.add))
            for k, oh in enumerate((oh1, oh2)):
                link(V.reduce_max(rs[:, 0, :], bi, axis=AX))
                link(V.tensor_tensor(t1, bi, bc(rs[:, 0, :]), ALU.is_equal))
                link(V.tensor_tensor(t1, t1, down, ALU.mult))
                link(V.reduce_max(rs[:, 1, :], t1, axis=AX))
                link(V.tensor_tensor(oh, down, bc(rs[:, 1, :]), ALU.is_equal))
                if k == 0:
                    link(V.scalar_tensor_tensor(bi, oh, -3.0e38, bi, ALU.mult, ALU.add))
            V.tensor_tensor(chosen[:, :, :], oh1, oh2, ALU.add).then_inc(s_mask, 1)
            for k, oh in enumerate((oh1, oh2)):
                link(V.tensor_tensor(t1, sc, oh, ALU.mult))
                link(V.reduce_sum(weight[:, :, k], t1, axis=AX))

            def places():
                cnt, nt, end, start = (sizes[:, i, :] for i in range(4))
                for e in range(E):
                    last = V.tensor_tensor_scan(cum[:, :, e], ones_sb[:, 0:NT], ranks[:, 1, :, e], 0.0, ALU.mult, ALU.add)
                link(last)
                link(V.tensor_copy(cnt, cum[:, NT - 1, :]))
                link(V.tensor_tensor(cmp_sz[:, :, :], cnt.unsqueeze(2).to_broadcast([P, E, E]),
                                     steps_sb[:, E:2 * E].unsqueeze(1).to_broadcast([P, E, E]), ALU.is_gt))
                link(V.reduce_sum(nt, cmp_sz[:, :, :], axis=AX))
                link(V.tensor_tensor_scan(end, ones_sb[:, 0:E], nt, 0.0, ALU.mult, ALU.add))
                link(V.tensor_tensor(start, end, nt, ALU.subtract))
                link(V.tensor_scalar(start, start, float(CH), None, ALU.mult))
                link(V.tensor_tensor(at, cum, ranks[:, 1, :, :], ALU.subtract))
                link(V.tensor_tensor(at, at, ranks[:, 0, :, :], ALU.add))
                link(V.tensor_tensor(at, at, over_tokens(start), ALU.add))
                for k, oh in enumerate((oh1, oh2)):
                    link(V.tensor_tensor(t1, at, oh, ALU.mult))
                    link(V.reduce_sum(posf[:, :, k], t1, axis=AX))
                V.tensor_copy(pos[:, :, :], posf[:, :, :]).then_inc(s_pos, 1)
                link(V.tensor_tensor(tile_c[:, :, :], steps_sb[0:1, 2 * E:2 * E + ST].unsqueeze(2).to_broadcast([1, ST, E]),
                                     end[0:1, :].unsqueeze(1).to_broadcast([1, ST, E]), ALU.is_ge))
                link(V.reduce_sum(tile_f[:, :], tile_c[:, :, :], axis=AX))
                link(V.tensor_scalar(tile_f[:, :], tile_f[:, :], float(E - 1), 1.0, ALU.min, ALU.add))
                V.tensor_copy(tile_slot[:, :], tile_f[:, :]).then_inc(s_pos, 1)

            def output(it, c):
                dve.wait_ge(s_pv, it * 2 + (c + 1))
                V.tensor_copy(o_sb[:, c, :], bank(6 + c)).then_inc(s_osb, 1)
                copy_v(c, ((it + 1) // (NCH // 2)) % H)
                dve.wait_ge(s_red, it * 2 + (c + 1))
                o = bank(6 + c).rearrange("p (t j w) -> p t w j", t=TPC, j=P // VW)[:, :, 0:VC, :]
                V.reduce_sum(o_n[:, c, :, :], o, axis=AX).then_inc(s_norm, 1)
                dve.wait_ge(s_norm, it * 2 + (c + 1))
                V.reciprocal(rec[:, c, :], o_n[:, c, :, HD]).then_inc(s_loop_a, 1)
                dve.wait_ge(s_loop_a, it * 6 + (3 * c + 1))
                V.tensor_tensor(o_n[:, c, :, 0:HD], o_n[:, c, :, 0:HD], rec[:, c, :].unsqueeze(2).to_broadcast([P, TPC, HD]),
                                ALU.mult).then_inc(s_loop_a, 1)
                dve.wait_ge(s_loop_a, it * 6 + (3 * c + 2))
                dst = resid[:, ds(((it % (NCH // 2)) * 2 + c) * TPC, TPC), ds((it // (NCH // 2)) * HD, HD)]
                V.tensor_tensor(dst, dst, o_n[:, c, :, 0:HD], ALU.add).then_inc(s_loop_a, 1)

            output(0, 0)
            dve.wait_ge(s_pre, 1)
            V.tensor_copy(ranks[:, :, :, :].rearrange("p a t e -> p (a t e)"), bank(6)).then_inc(s_prc, 1)
            dve.wait_ge(s_prc, 1)
            output(0, 1)
            places()
            with dve.Fori(1, ITERS) as it:
                for c in range(2):
                    output(it, c)
            dve.wait_ge(s_loop_a, ITERS * 6)

            dve.wait_ge(s_scat, 16 * NT * TOP)
            V.memset(hid_hi[FT[2]:FT[2] + 1, 2, :].bitcast(f32), 1.0)
            V.memset(hid_lo[FT[2]:FT[2] + 1, 2, :].bitcast(f32), 0.0).then_inc(s_one, 1)
            dve.wait_ge(s_one, 1)

            def tokens_lo(m, half, chunk=None):
                dve.wait_ge(s_xhi, m + 1)
                if chunk is None:
                    src, hi, dst = bank(4, 2), x_hi[:, half, :].bitcast(f32), x_lo[:, half, :]
                else:
                    src = xnT[:, :, ds(chunk * CH, CH)]
                    hi = x_hi[:, half, :].bitcast(f32).rearrange("p (t n) -> p t n", t=DT)
                    dst = x_lo[:, half, :].rearrange("p (t n) -> p t n", t=DT)
                V.tensor_tensor(dst, src, hi, ALU.subtract).then_inc(s_xboth, 1)

            def weights13_lo(m, half):
                dve.wait_ge(s_w13h, m + 1)
                V.tensor_tensor(w_lo[:, half, 0:2 * DT * F], w_raw[:, half, 0:2 * DT * F],
                                w_hi[:, half, 0:2 * DT * F].bitcast(f32), ALU.subtract).then_inc(s_w13, 1)

            def weights2_lo(m, half):
                dve.wait_ge(s_w2h, m + 1)
                V.tensor_tensor(w_lo[:, half, 2 * DT * F:WHALF], w_raw[:, half, 2 * DT * F:WHALF],
                                w_hi[:, half, 2 * DT * F:WHALF].bitcast(f32), ALU.subtract).then_inc(s_w2, 1)

            def product(m, half, bhalf, j, first=False):
                dve.wait_ge(s_gin, m * 3 + (j + 1))
                if not first or j == 2:
                    dve.wait_ge(s_hid, m * 3 + (j - 1))
                V.scalar_tensor_tensor(prod[0:FT[j], j % 2, :], up_bank(1, half, j)[0:FT[j], :], bias_sb[0:FT[j], bhalf, 3 + j:4 + j],
                                       gate_in[0:FT[j], j % 2, :], ALU.add, ALU.mult).then_inc(s_prod, 1)

            def hidden_lo(m, j):
                dve.wait_ge(s_hhi, m * 3 + (j + 1))
                V.tensor_tensor(hid_lo[0:FT[j], j, :], hid[0:FT[j], j % 2, :], hid_hi[0:FT[j], j, :].bitcast(f32),
                                ALU.subtract).then_inc(s_hlo, 1)

            def keep(m, half, wait=True):
                dve.wait_ge(s_y, m + 1)
                if wait:
                    dve.wait_ge(s_yst[half], (m // 2) * 16)
                V.tensor_copy(y_sb[:, half, :, :].rearrange("p t n -> p (t n)"), bank(6, 2)).then_inc(s_yc, 1)

            def add_shared(c):
                dve.wait_ge(s_y, c + (ST + 1))
                dst = resid[:, ds(c * TPC, TPC), :].rearrange("p t n -> p (t n)")
                V.tensor_tensor(dst, dst, bank(6, 2), ALU.add).then_inc(s_yc, 1)
                dve.wait_ge(s_yc, c + (ST + 1))

            def combine(c):
                b = c % 3
                dve.wait_ge(s_got[b], (c // 3 + 1) * (16 * TPC * TOP))
                for k in range(TOP):
                    for t in range(TPC):
                        row = resid[:, c * TPC + t, :]
                        last = V.scalar_tensor_tensor(row, got[b][:, t, k, :], weight[:, c * TPC + t, k:k + 1], row, ALU.mult, ALU.add)
                    if k == 0:
                        last.then_inc(s_sum, 1)
                        dve.wait_ge(s_sum, c + 1)
                last.then_inc(s_used, 1)
                dve.wait_ge(s_used, c + 1)

            def work(m, half, bhalf, output, chunk=None, tokens=True, weights=True, first=False):
                if tokens:
                    tokens_lo(m + 1, 1 - half, chunk)
                if weights:
                    weights13_lo(m + 1, 1 - half)
                product(m, half, bhalf, 0, first)
                product(m, half, bhalf, 1, first)
                output()
                hidden_lo(m, 0)
                if weights:
                    weights2_lo(m + 1, 1 - half)
                hidden_lo(m, 1)
                product(m, half, bhalf, 2, first)
                hidden_lo(m, 2)

            SW = ST % 2
            weights13_lo(0, 0)
            tokens_lo(0, 0)
            weights2_lo(0, 0)
            work(0, 0, 0, lambda: None, first=True)
            work(1, 1, 1, lambda: keep(0, 0, wait=False))
            work(2, 0, 0, lambda: keep(1, 1, wait=False))
            with dve.Fori(1, (ST - 3) // 2) as p:
                work(p * 2 + 1, 1, 1, lambda: keep(p * 2, 0))
                work(p * 2 + 2, 0, 0, lambda: keep(p * 2 + 1, 1))
            work(ST - 2, 1, 1, lambda: keep(ST - 3, 0))
            work(ST - 1, 0, 0, lambda: keep(ST - 2, 1), chunk=0)
            for c in range(NCH):
                work(ST + c, (ST + c) % 2, SW, lambda: add_shared(c - 1) if c else keep(ST - 1, 0),
                     chunk=c + 1, tokens=(c < NCH - 1), weights=False)
                if c >= 1:
                    combine(c - 1)
            combine(NCH - 1)
            add_shared(NCH - 1)


def kernel(**inputs):
    import numpy as np
    import concourse.bacc as bacc
    from concourse import mybir as mb
    from concourse.bass_utils import run_bass_kernel_spmd

    a = {k[3:]: np.ascontiguousarray(v) for k, v in inputs.items()}

    def columns(shared, routed):
        b = np.concatenate([shared[None], routed], 0)
        full = np.zeros((NS, 3 * P), b.dtype)
        full[:, :F] = b
        return full.reshape(NS, 3, P).transpose(0, 2, 1)

    def slots(shared, routed):
        return np.concatenate([shared[None], routed], 0)

    hones = np.zeros((P, DT, H), np.float32)
    for p in range(P):
        for t in range(DT):
            hones[p, t, t * (P // HD) + p // HD] = 1.0
    arrays = {
        "x": a["attn_x"], "wqT": np.ascontiguousarray(a["attn_Wq"].T), "wkT": np.ascontiguousarray(a["attn_Wk"].T),
        "wvT": np.ascontiguousarray(a["attn_Wv"].T), "gT": np.ascontiguousarray(a["ffn_gate_w"].T), "gate_b": a["ffn_gate_b"],
        "w1": slots(a["ffn_sw1"], a["ffn_w1"]), "w3": slots(a["ffn_sw3"], a["ffn_w3"]), "w2": slots(a["ffn_sw2"], a["ffn_w2"]),
        "b13": np.ascontiguousarray(np.concatenate([columns(a["ffn_sb1"], a["ffn_b1"]), columns(a["ffn_sb3"], a["ffn_b3"])], 2)),
        "b2": slots(a["ffn_sb2"], a["ffn_b2"]),
        "ident": np.eye(P, dtype=np.float32), "hones": hones,
        "prefix": np.triu(np.ones((P, P), np.float32), 1), "ones": np.ones((P, P), np.float32),
        "steps": np.concatenate([E - np.arange(E), CH * np.arange(E), np.arange(ST)]).astype(np.float32),
    }
    nc = bacc.Bacc("TRN2", target_bir_lowering=False, num_devices=1)
    aps = [nc.dram_tensor("in_" + n, v.shape, mb.dt.from_np(v.dtype), kind="ExternalInput").ap() for n, v in arrays.items()]
    out = nc.dram_tensor("out_0", (1, T, D), mb.dt.float32, kind="ExternalOutput").ap()
    layer_program(nc, *aps, out)
    r = run_bass_kernel_spmd(nc, [{"in_" + n: v for n, v in arrays.items()}], core_ids=[0])
    return r.results[0]["out_0"]
```
